# Optimizing a Trainium2 kernel written in Bass

```python
import numpy as np
import jax
import jax.numpy as jnp

def _softmax(x, axis=-1):
    return jax.nn.softmax(x, axis=axis)

def _gelu(x):
    return jax.nn.gelu(x, approximate=True)

def _silu(x):
    return jax.nn.silu(x)

def _sigmoid(x):
    return jax.nn.sigmoid(x)

def _layernorm(x, axis=-1, eps=1e-05):
    m = jnp.mean(x, axis=axis, keepdims=True)
    v = jnp.var(x, axis=axis, keepdims=True)
    return (x - m) / jnp.sqrt(v + eps)

def _scatter_add(tgt, idx, src, axis=0):
    return tgt.at[idx].add(src)

def _segment_sum(src, seg, n):
    return jax.ops.segment_sum(src, seg, n)
kernel_name = 'mk_macaron_d1_jaxref_r8_17dc33'

def setup_inputs(seed: int=0):
    np.random.seed(seed)
    _w = jnp.asarray

    def _L0_attn_setup():
        import jax, jax.numpy as jnp
        import numpy as np
        B, T, C, R = (8, 128, 128, 64)
        EPS = 1e-05
        key = jax.random.key(seed)
        ks = jax.random.split(key, 8)
        x = jax.random.normal(ks[0], (B, T, C), dtype=jnp.float32)
        W_attn = jax.random.normal(ks[1], (3 * C, C), dtype=jnp.float32) * 0.02
        W_proj = jax.random.normal(ks[2], (C, C), dtype=jnp.float32) * 0.02
        lora_attn_A = jax.random.normal(ks[3], (C, R), dtype=jnp.float32) * 0.02
        lora_attn_B = jax.random.normal(ks[4], (R, 3 * C), dtype=jnp.float32) * 0.02
        lora_proj_A = jax.random.normal(ks[5], (C, R), dtype=jnp.float32) * 0.02
        lora_proj_B = jax.random.normal(ks[6], (R, C), dtype=jnp.float32) * 0.02
        bn_gamma = jnp.ones((3 * C,), dtype=jnp.float32)
        bn_beta = jnp.zeros((3 * C,), dtype=jnp.float32)
        return {'x': x, 'W_attn': W_attn, 'W_proj': W_proj, 'lora_attn_A': lora_attn_A, 'lora_attn_B': lora_attn_B, 'lora_proj_A': lora_proj_A, 'lora_proj_B': lora_proj_B, 'bn_gamma': bn_gamma, 'bn_beta': bn_beta}
    _L0_attn_in = _L0_attn_setup()

    def _L0_ffn_setup():
        import jax, jax.numpy as jnp
        import numpy as np
        TOP_K = 8
        NUM_EXPERTS = 32
        HIDDEN = 128
        EXPERT_DIM = 64
        key = jax.random.key(seed)
        k1, k2, k3, k4 = jax.random.split(key, 4)
        hidden_states = jax.random.normal(k1, (1, 256, HIDDEN), dtype=jnp.float32)
        gate_w = jax.random.normal(k2, (NUM_EXPERTS, HIDDEN), dtype=jnp.float32) * 0.02
        gate_up_w = jax.random.normal(k3, (NUM_EXPERTS, 2 * EXPERT_DIM, HIDDEN), dtype=jnp.float32) * 0.02
        down_w = jax.random.normal(k4, (NUM_EXPERTS, HIDDEN, EXPERT_DIM), dtype=jnp.float32) * 0.02
        return {'hidden_states': hidden_states, 'gate_w': gate_w, 'gate_up_w': gate_up_w, 'down_w': down_w}
    _L0_ffn_in = _L0_ffn_setup()
    _d = {'L0_attn_x': _L0_attn_in['x'], 'L0_attn_W_attn': _L0_attn_in['W_attn'], 'L0_attn_W_proj': _L0_attn_in['W_proj'], 'L0_attn_lora_attn_A': _L0_attn_in['lora_attn_A'], 'L0_attn_lora_attn_B': _L0_attn_in['lora_attn_B'], 'L0_attn_lora_proj_A': _L0_attn_in['lora_proj_A'], 'L0_attn_lora_proj_B': _L0_attn_in['lora_proj_B'], 'L0_attn_bn_gamma': _L0_attn_in['bn_gamma'], 'L0_attn_bn_beta': _L0_attn_in['bn_beta'], 'L0_ffn_gate_w': _L0_ffn_in['gate_w'], 'L0_ffn_gate_up_w': _L0_ffn_in['gate_up_w'], 'L0_ffn_down_w': _L0_ffn_in['down_w']}
    _x0 = _d['L0_attn_x']
    _d['L0_attn_x'] = jax.random.normal(jax.random.fold_in(jax.random.key(seed), 1), (8, 512, 128), dtype=_x0.dtype)
    del _x0
    return _d

def reference(L0_attn_x, L0_attn_W_attn, L0_attn_W_proj, L0_attn_lora_attn_A, L0_attn_lora_attn_B, L0_attn_lora_proj_A, L0_attn_lora_proj_B, L0_attn_bn_gamma, L0_attn_bn_beta, L0_ffn_gate_w, L0_ffn_gate_up_w, L0_ffn_down_w):

    def _L0_attn_ref(x, W_attn, W_proj, lora_attn_A, lora_attn_B, lora_proj_A, lora_proj_B, bn_gamma, bn_beta):
        import jax, jax.numpy as jnp
        import numpy as np
        B, T, C, R = (8, 128, 128, 64)
        EPS = 1e-05
        Bb, Tt, Cc = x.shape
        Wm_attn = W_attn + (lora_attn_A @ lora_attn_B).reshape(W_attn.shape)
        xa = jnp.einsum('btc,dc->btd', x, Wm_attn)
        mean = xa.mean(axis=(0, 1))
        var = xa.var(axis=(0, 1))
        xa = (xa - mean) * jax.lax.rsqrt(var + EPS) * bn_gamma + bn_beta
        q, k, v = jnp.split(xa, 3, axis=-1)
        scale = 1.0 / jnp.sqrt(jnp.asarray(Cc, dtype=x.dtype))
        att = jnp.einsum('btc,bsc->bts', q, k) * scale
        causal = jnp.tril(jnp.ones((Tt, Tt), dtype=bool))
        att = jnp.where(causal[None, :, :], att, -jnp.inf)
        att = jax.nn.softmax(att, axis=-1)
        y = jnp.einsum('bts,bsc->btc', att, v)
        y = jnp.einsum('btc,dc->btd', y, W_proj)
        Wm_proj = W_proj + (lora_proj_A @ lora_proj_B).reshape(W_proj.shape)
        y = jnp.einsum('btc,dc->btd', y, Wm_proj)
        return y

    def _L0_ffn_ref(hidden_states, gate_w, gate_up_w, down_w):
        import jax, jax.numpy as jnp
        import numpy as np
        TOP_K = 8
        NUM_EXPERTS = 32
        HIDDEN = 128
        EXPERT_DIM = 64
        B, S, H = hidden_states.shape
        x = hidden_states.reshape(-1, H)
        logits = x @ gate_w.T
        probs = jax.nn.softmax(logits.astype(jnp.float32), axis=-1)
        top_w, top_idx = jax.lax.top_k(probs, TOP_K)
        top_w = top_w / jnp.sum(top_w, axis=-1, keepdims=True)
        top_w = top_w.astype(x.dtype)
        comb = jnp.sum(jax.nn.one_hot(top_idx, NUM_EXPERTS, dtype=x.dtype) * top_w[..., None], axis=1)

        def body(acc, ws):
            guw, dw, w_e = ws
            gu = x @ guw.T
            g, u = jnp.split(gu, 2, axis=-1)
            y = u * jax.nn.silu(g) @ dw.T
            return (acc + y * w_e[:, None], None)
        init = jnp.zeros_like(x)
        out, _ = jax.lax.scan(body, init, (gate_up_w, down_w, comb.T))
        return out.reshape(B, S, H)
    x = L0_attn_x
    x = x + 0.5 * _L0_ffn_ref(_layernorm(x, axis=-1), L0_ffn_gate_w, L0_ffn_gate_up_w, L0_ffn_down_w)
    x = x + _L0_attn_ref(_layernorm(x, axis=-1), L0_attn_W_attn, L0_attn_W_proj, L0_attn_lora_attn_A, L0_attn_lora_attn_B, L0_attn_lora_proj_A, L0_attn_lora_proj_B, L0_attn_bn_gamma, L0_attn_bn_beta)
    x = x + 0.5 * _L0_ffn_ref(_layernorm(x, axis=-1), L0_ffn_gate_w, L0_ffn_gate_up_w, L0_ffn_down_w)
    return x

_drawn_inputs = setup_inputs


def setup_inputs(seed=0):
    import zlib

    import numpy as np

    out = dict(_drawn_inputs(seed))
    spreads = {'L0_attn_bn_gamma': (1.0, 0.6), 'L0_attn_bn_beta': (0.0, 0.8)}
    factors = {'L0_attn_W_attn': 5.479,
     'L0_attn_W_proj': 4.777,
     'L0_attn_lora_attn_A': 8.0,
     'L0_attn_lora_attn_B': 8.0,
     'L0_attn_lora_proj_A': 8.0,
     'L0_attn_lora_proj_B': 8.0,
     'L0_ffn_gate_w': 8.0,
     'L0_ffn_gate_up_w': 8.0,
     'L0_ffn_down_w': 8.0}
    for name, (base, spread) in spreads.items():
        noise = np.random.default_rng([zlib.crc32(name.encode()), seed]).standard_normal(out[name].shape)
        drawn = base * np.exp(spread * noise) if base else spread * noise
        out[name] = jnp.asarray(drawn.astype(out[name].dtype))
    for name, factor in factors.items():
        out[name] = (out[name] * factor).astype(out[name].dtype)
    return out
```

```python
from contextlib import ExitStack

import numpy as np

import concourse.bass as bass
from concourse import mybir

F32 = mybir.dt.float32
F32R = mybir.dt.float32r
ALU = mybir.AluOpType
ACT = mybir.ActivationFunctionType
AX_X = mybir.AxisListType.X

P = 128
TILES = 4
CHUNK = TILES * P
CHUNKS = 8
EXPERTS = 32
EDIM = 64
PAIRS = EXPERTS // 2
TOPK = 8
EPS = 1e-5
MASKED = -1e30
LAG = 3
GROUP = 4
HSPLIT = 4
UNROLL = 2


def after(eng, sem, value):
    if not isinstance(value, int) or value > 0:
        eng.wait_ge(sem, value)


def hold(eng, sem, value):
    if isinstance(value, int):
        after(eng, sem, value)
    else:
        eng.wait_ge(sem, value)
        eng.nop(nofuse=True)


def rows(x_sb, c):
    return x_sb[:, TILES * c:TILES * c + TILES, :] if isinstance(c, int) else x_sb[:, bass.ds(TILES * c, TILES), :]


def setup_block(nc, d, w, x_sb, bank):
    with ExitStack() as ctx:
        def sb(name, shape, dt=F32):
            return ctx.enter_context(nc.sbuf_tensor(name, shape, dt))

        def sem(name):
            return ctx.enter_context(nc.semaphore(name))

        gu_nat = sb("gu_nat", [P, EXPERTS, P])
        dn_nat = sb("dn_nat", [P, EXPERTS * EDIM])
        bn_nat = sb("bn_nat", [6, P])
        gate_nat = sb("gate_nat", [EXPERTS, P])
        attn_nat = sb("attn_nat", [P, 3, P])
        proj_nat = sb("proj_nat", [P, P])
        la_a = sb("la_a", [P, EDIM])
        lp_a = sb("lp_a", [P, EDIM])
        la_b = sb("la_b", [EDIM, 3 * P])
        lp_b = sb("lp_b", [EDIM, P])
        la_at = sb("la_at", [EDIM, P])
        lp_at = sb("lp_at", [EDIM, P])
        projm_t = sb("projm_t", [P, P])

        gu_in = [sem(f"gu_in{i}") for i in range(8)]
        dn_in = sem("dn_in")
        small_in = sem("small_in")
        x_in = sem("x_in")
        const_step = sem("const_step")
        turned = sem("turned")
        hi_made = sem("hi_made")
        lo_made = sem("lo_made")
        block = ctx.enter_context(nc.Block())

        UPS = 8
        DOWNS = 4
        GATE, LORA_AT, ATTN, DELTA, PROJM, COMB = range(UPS + DOWNS, UPS + DOWNS + 6)

        def at(n):
            return bank[:, n % 4, :]

        @block.sync
        def _(sp):
            for q in range(8):
                sp.dma_start(gu_nat[:, 4 * q:4 * q + 4, :],
                             d["gate_up"][4 * q:4 * q + 4].rearrange("e r h -> r e h")).then_inc(gu_in[q], 16)
            for q in range(CHUNKS):
                sp.dma_start(rows(x_sb, q), d["x"][q].rearrange("(n p) h -> p n h", p=P)).then_inc(x_in, 16)
            sp.wait_ge(x_in, 16 * CHUNKS)

        @block.scalar
        def _(act):
            act.dma_start(gate_nat[:], d["gate"]).then_inc(small_in, 16)
            act.dma_start(attn_nat[:], d["W_attn"].rearrange("(m p) c -> p m c", p=P)).then_inc(small_in, 16)
            act.dma_start(proj_nat[:], d["W_proj"]).then_inc(small_in, 16)
            act.dma_start(la_a[:], d["lora_attn_A"]).then_inc(small_in, 16)
            act.dma_start(lp_a[:], d["lora_proj_A"]).then_inc(small_in, 16)
            act.dma_start(la_b[:], d["lora_attn_B"]).then_inc(small_in, 16)
            act.dma_start(lp_b[:], d["lora_proj_B"]).then_inc(small_in, 16)
            act.dma_start(bn_nat[0:3, :], d["gamma"].rearrange("(m p) -> m p", p=P)).then_inc(small_in, 16)
            act.dma_start(bn_nat[3:6, :], d["beta"].rearrange("(m p) -> m p", p=P)).then_inc(small_in, 16)
            act.dma_start(dn_nat[:].rearrange("h (e k) -> h e k", e=EXPERTS),
                          d["down"].rearrange("e h k -> h e k")).then_inc(dn_in, 16)
            for q in range(UPS):
                act.wait_ge(turned, q + 1)
                t = at(q).rearrange("p (e r) -> p e r", e=4)
                for half, dst in enumerate((w["g_hi"], w["u_hi"])):
                    i = act.activation(dst[:, 2 * q:2 * q + 2, :].rearrange("p a (b k) -> p (a b) k", b=2),
                                       t[:, :, half * EDIM:half * EDIM + EDIM], ACT.Copy)
                i.then_inc(hi_made, 1)
            for q in range(DOWNS):
                act.wait_ge(turned, UPS + q + 1)
                act.activation(w["d_hi"][:, 4 * q:4 * q + 4, :].rearrange("p a b -> p (a b)"), at(UPS + q),
                               ACT.Copy).then_inc(hi_made, 1)
            act.wait_ge(turned, GATE + 1)
            act.activation(w["r_hi"][:], at(GATE)[:, 0:EXPERTS], ACT.Copy).then_inc(hi_made, 1)
            act.wait_ge(turned, LORA_AT + 1)
            act.activation(la_at[:], at(LORA_AT)[0:EDIM, 0:P], ACT.Copy)
            act.activation(lp_at[:], at(LORA_AT)[0:EDIM, P:2 * P], ACT.Copy).then_inc(hi_made, 1)
            act.wait_ge(turned, ATTN + 1)
            act.activation(w["gamma_beta"][:], at(ATTN)[:, 3 * P:3 * P + 6], ACT.Copy)
            act.activation(w["qkv_t"][:], at(ATTN)[:, 0:3 * P], ACT.Copy).then_inc(hi_made, 1)
            act.wait_ge(turned, PROJM + 1)
            act.activation(projm_t[:], at(PROJM)[:, 0:P], ACT.Copy).then_inc(hi_made, 1)
            act.wait_ge(turned, COMB + 1)
            act.activation(w["out_t"][:], at(COMB)[:, 0:P], ACT.Copy).then_inc(hi_made, 1)

        @block.vector
        def _(dve):
            for q in range(UPS):
                dve.wait_ge(hi_made, q + 1)
                t = at(q).rearrange("p (e r) -> p e r", e=4)
                for half, (hi, lo) in enumerate(((w["g_hi"], w["g_lo"]), (w["u_hi"], w["u_lo"]))):
                    s = slice(2 * q, 2 * q + 2)
                    i = dve.tensor_tensor(lo[:, s, :].rearrange("p a (b k) -> p (a b) k", b=2),
                                          t[:, :, half * EDIM:half * EDIM + EDIM],
                                          hi[:, s, :].bitcast(F32).rearrange("p a (b k) -> p (a b) k", b=2),
                                          ALU.subtract)
                i.then_inc(lo_made, 1)
            for q in range(DOWNS):
                dve.wait_ge(hi_made, UPS + q + 1)
                dve.tensor_tensor(w["d_lo"][:, 4 * q:4 * q + 4, :].rearrange("p a b -> p (a b)"), at(UPS + q),
                                  w["d_hi"][:, 4 * q:4 * q + 4, :].bitcast(F32).rearrange("p a b -> p (a b)"),
                                  ALU.subtract).then_inc(lo_made, 1)
            dve.wait_ge(hi_made, GATE + 1)
            dve.tensor_tensor(w["r_lo"][:], at(GATE)[:, 0:EXPERTS], w["r_hi"][:].bitcast(F32),
                              ALU.subtract).then_inc(lo_made, 1)
            dve.wait_ge(hi_made, ATTN + 1)
            dve.wait_ge(turned, DELTA + 1)
            qkv = w["qkv_t"][:].rearrange("c (r j) -> c r j", j=3)
            dve.tensor_tensor(qkv, at(DELTA)[:, 0:3 * P].rearrange("c (j r) -> c r j", j=3), qkv,
                              ALU.add).then_inc(lo_made, 1)

        @block.gpsimd
        def _(pool):
            pool.memset(w["ident"][:], 0.0).then_inc(const_step, 1)
            pool.wait_ge(const_step, 1)
            pool.affine_select(out=w["ident"][:], in_=w["ident"][:], compare_op=ALU.not_equal, fill=1.0, base=0,
                               pattern=[[-1, P]], channel_multiplier=1).then_inc(const_step, 1)
            pool.memset(w["neg_half"][:], -0.5)
            pool.memset(w["eps"][:], EPS)
            pool.memset(w["causal"][:], 0.0).then_inc(const_step, 1)
            pool.wait_ge(const_step, 3)
            pool.affine_select(out=w["causal"][:], in_=w["causal"][:], compare_op=ALU.is_ge, fill=-MASKED, base=0,
                               pattern=[[-1, P]], channel_multiplier=1).then_inc(const_step, 1)
            pool.wait_ge(const_step, 4)
            pool.tensor_copy(w["causal_b"][:], w["causal"][:])
            pool.tensor_copy(w["ident_b"][:], w["ident"][:]).then_inc(const_step, 1)

        @block.tensor
        def _(pe):
            ident = w["ident"]
            pe.wait_ge(const_step, 2)
            for q in range(UPS):
                pe.wait_ge(gu_in[q], 16)
                if q >= 4:
                    pe.wait_ge(lo_made, q - 3)
                for e in range(4):
                    i = pe.transpose(at(q)[:, e * P:e * P + P], gu_nat[:, 4 * q + e, :], ident[:])
                i.then_inc(turned, 1)
            pe.wait_ge(dn_in, 16)
            for q in range(DOWNS):
                pe.wait_ge(lo_made, UPS + q - 3)
                for e in range(4):
                    n = 4 * q + e
                    i = pe.transpose(at(UPS + q)[:, e * P:e * P + P], dn_nat[:, n * P:n * P + P], ident[:])
                i.then_inc(turned, 1)
            pe.wait_ge(small_in, 16 * 9)
            pe.wait_ge(lo_made, GATE - 3)
            pe.transpose(at(GATE)[:, 0:EXPERTS], gate_nat[:], ident[0:EXPERTS, 0:EXPERTS]).then_inc(turned, 1)
            pe.wait_ge(lo_made, LORA_AT - 3)
            pe.transpose(at(LORA_AT)[0:EDIM, 0:P], la_a[:], ident[:])
            pe.transpose(at(LORA_AT)[0:EDIM, P:2 * P], lp_a[:], ident[:]).then_inc(turned, 1)
            pe.wait_ge(lo_made, ATTN - 3)
            for m in range(3):
                pe.transpose(at(ATTN)[:, m * P:m * P + P], attn_nat[:, m, :], ident[:])
            i = pe.transpose(at(ATTN)[:, 3 * P:3 * P + 6], bn_nat[:], ident[0:6, 0:6])
            i.then_inc(turned, 1)
            pe.wait_ge(lo_made, DELTA - 3)
            pe.wait_ge(hi_made, LORA_AT + 1)
            for j in range(3):
                i = pe.matmul(at(DELTA)[:, j * P:j * P + P], la_b[:, j * P:j * P + P], la_at[:], start=True, stop=True)
            i.then_inc(turned, 1)
            pe.wait_ge(lo_made, GATE + 1)
            pe.matmul(at(PROJM)[:, 0:P], proj_nat[:], ident[:], start=True, stop=False)
            pe.matmul(at(PROJM)[:, 0:P], lp_b[:], lp_at[:], start=False, stop=True).then_inc(turned, 1)
            pe.wait_ge(hi_made, PROJM)
            pe.matmul(at(COMB)[:, 0:P], proj_nat[:], projm_t[:], start=True, stop=True).then_inc(turned, 1)


def ffn_block(nc, w, x_sb, bank, qkv, out):
    with ExitStack() as ctx:
        tag = "a" if qkv else "c"

        def sb(name, shape, dt=F32):
            return ctx.enter_context(nc.sbuf_tensor(f"{name}_{tag}", shape, dt))

        def sem(name):
            return ctx.enter_context(nc.semaphore(f"{name}_{tag}"))

        def ln_set(name):
            return {
                "stats": sb(f"{name}_stats", [P, TILES, 6]), "mv": sb(f"{name}_mv", [P, TILES, 2]),
                "ve": sb(f"{name}_ve", [P, TILES, 1]), "rstd": sb(f"{name}_rstd", [P, TILES, 1]),
                "xn": sb(f"{name}_xn", [P, TILES, P]),
                "stats_made": sem(f"{name}_stats_made"), "mv_made": sem(f"{name}_mv_made"),
                "ve_made": sem(f"{name}_ve_made"), "rstd_made": sem(f"{name}_rstd_made"),
                "xn_made": sem(f"{name}_xn_made"),
            }

        ln_f = ln_set("lnf")
        ln_q = ln_set("lnq") if qkv else None
        x_t = sb("x_t", [P, 2, 2, CHUNK], F32R)
        comb_t = sb("comb_t", [EXPERTS, CHUNK])
        share = sb("share", [P, 2, GROUP, CHUNK])
        comb_d = nc.dram_tensor(f"comb_{tag}", [2, EXPERTS, CHUNK], F32, kind="Internal").ap()
        scaled = sb("scaled", [P, 2, CHUNK])
        hid = sb("hid", [P, 2, CHUNK])
        hid_hi = sb("hid_hi", [P, HSPLIT, CHUNK], F32R)
        hid_lo = sb("hid_lo", [P, HSPLIT, CHUNK], F32R)
        y_sb = sb("y_sb", [P, CHUNK])
        logits = sb("logits", [P, TILES, EXPERTS])
        rest = sb("rest", [P, TILES, EXPERTS])
        top = sb("top", [P, TILES, TOPK])
        z = sb("z", [P, TILES, EXPERTS])
        chosen = sb("chosen", [P, TILES, EXPERTS])
        th = sb("th", [P, TILES, EXPERTS])
        den = sb("den", [P, TILES, EXPERTS])
        den_inv = sb("den_inv", [P, TILES, EXPERTS])
        num = sb("num", [P, TILES, EXPERTS])
        wt = sb("wt", [P, TILES, EXPERTS])
        wn = sb("wn", [P, TILES, EXPERTS])
        wsum = sb("wsum", [P, TILES, 1])
        winv = sb("winv", [P, TILES, 1])
        if qkv:
            x2_t = sb("x2_t", [P, CHUNK])
            v_t = sb("v_t", [P, CHUNK])

        gate_ready = sem("gate_ready")
        up_ready = sem("up_ready")
        silu_made = sem("silu_made")
        scaled_made = sem("scaled_made")
        hid_made = sem("hid_made")
        comb_stored = sem("comb_stored")
        share_in = [sem(f"share_in{i}") for i in range(2)]
        hi_made = sem("hi_made")
        lo_made = sem("lo_made")
        down_done = sem("down_done")
        y_made = sem("y_made")
        misc_ready = sem("misc_ready")
        misc_read = sem("misc_read")
        misc_half = sem("misc_half")
        top_made = sem("top_made")
        rest_made = sem("rest_made")
        z_made = sem("z_made")
        chosen_made = sem("chosen_made")
        th_made = sem("th_made")
        den_made = sem("den_made")
        den_inv_made = sem("den_inv_made")
        num_made = sem("num_made")
        wt_made = sem("wt_made")
        wsum_made = sem("wsum_made")
        winv_made = sem("winv_made")
        wn_made = sem("wn_made")
        proj_stats_made = sem("proj_stats_made")
        stored = sem("stored")
        block = ctx.enter_context(nc.Block())

        GATE_BANK, UP_BANK, Y_BANK, MISC_BANK = 0, 2, 4, 7
        misc = bank[:, MISC_BANK, :]

        NEXT, PREV = 1, -1
        STEPS = [("turn_x", 3, NEXT), ("route", 4, NEXT), ("add", 5, PREV), ("turn_w", 9, NEXT)]
        STEPS += [("turn_n", 10, PREV), ("q", 11, PREV), ("k", 12, PREV), ("v", 13, PREV),
                  ("turn_v", 14, PREV)] if qkv else []
        N_NEXT = sum(s[2] == NEXT for s in STEPS)
        N_PREV = len(STEPS) - N_NEXT

        def there(step, c):
            if not isinstance(c, int):
                return True
            return c >= 1 if step[2] == PREV else c <= CHUNKS - 2

        def before(c):
            if isinstance(c, int) and c < 1:
                return 0 if c < 0 else N_NEXT
            if isinstance(c, int) and c == CHUNKS:
                return before(c - 1) + N_PREV
            return 2 * N_NEXT + (c - 1) * (N_NEXT + N_PREV)

        def count(name, c):
            return before(c) + ([s[0] for s in STEPS if there(s, c)].index(name) + 1)

        def on_chunks(eng, slot):
            for p in range(PAIRS):
                slot(0, 0, p)
            with eng.Fori(0, (CHUNKS - 2) // UNROLL) as k:
                for u in range(1, 1 + UNROLL):
                    for p in range(PAIRS):
                        slot(k * UNROLL + u, u % 2, p)
            for p in range(PAIRS):
                slot(CHUNKS - 1, (CHUNKS - 1) % 2, p)

        def steps_at(c, p, late):
            return [s[0] for s in STEPS if s[1] == p - late and there(s, c)]

        first_steps = [s[0] for s in STEPS if s[2] == NEXT]
        last_steps = [s[0] for s in STEPS if s[2] == PREV]

        def is_first(c):
            return isinstance(c, int) and c == 0

        @block.tensor
        def _(pe):
            ident = w["ident"]

            def three(dst, hi, lo, x_hi, x_lo, start, stop):
                pe.matmul(dst, hi, x_hi, start=start, stop=False)
                pe.matmul(dst, hi, x_lo, start=False, stop=False)
                return pe.matmul(dst, lo, x_hi, start=False, stop=stop)

            def down(c, par, p):
                g = PAIRS * c + p
                if p == 0:
                    after(pe, y_made, c - 1)
                after(pe, hi_made, g + 1)
                after(pe, lo_made, g + 1)
                b = p % HSPLIT
                three(bank[:, Y_BANK + par, :], w["d_hi"][:, p, :], w["d_lo"][:, p, :], hid_hi[:, b, :], hid_lo[:, b, :],
                      p == 0, p == PAIRS - 1).then_inc(down_done, 1)

            def step(name, c, par):
                nxt = 1 - par
                after(pe, misc_read, count(name, c) - 1)
                if name == "add":
                    after(pe, y_made, c)
                    for i in range(TILES):
                        last = pe.transpose(misc[:, i * P:i * P + P], y_sb[:, i * P:i * P + P], ident[:])
                elif name in ("turn_x", "turn_n"):
                    ln, k = (ln_f, c + 2) if name == "turn_x" else (ln_q, c)
                    after(pe, ln["xn_made"], k)
                    for i in range(TILES):
                        last = pe.transpose(misc[:, i * P:i * P + P], ln["xn"][:, i, :], ident[:])
                elif name == "route":
                    for i in range(TILES):
                        s = slice(i * P, i * P + P)
                        o = misc[:, i * EXPERTS:(i + 1) * EXPERTS]
                        pe.matmul(o, x_t[:, nxt, 0, s], w["r_hi"][:], start=True, stop=False)
                        pe.matmul(o, x_t[:, nxt, 1, s], w["r_hi"][:], start=False, stop=False)
                        last = pe.matmul(o, x_t[:, nxt, 0, s], w["r_lo"][:], start=False, stop=True)
                elif name in "qkv":
                    m = "qkv".index(name)
                    last = pe.matmul(misc, w["qkv_t"][:, m * P:m * P + P], x2_t[:], start=True, stop=True)
                elif name == "turn_w":
                    after(pe, wn_made, c + 2)
                    for i in range(TILES):
                        last = pe.transpose(misc[0:EXPERTS, i * P:i * P + P], wn[:, i, :], ident[:])
                elif name == "turn_v":
                    for i in range(TILES):
                        last = pe.transpose(misc[:, i * P:i * P + P], v_t[:, i * P:i * P + P], ident[:])
                last.then_inc(misc_ready, 1)

            def slot(c, par, p):
                g = PAIRS * c + p
                b = p % 2
                x_hi, x_lo = x_t[:, par, 0, :], x_t[:, par, 1, :]
                if p == 0:
                    after(pe, misc_read, before(c))
                after(pe, scaled_made, g - 1)
                three(bank[:, UP_BANK + b, :], w["u_hi"][:, p, :], w["u_lo"][:, p, :],
                      x_hi, x_lo, True, True).then_inc(up_ready, 1)
                after(pe, hid_made, g - 1)
                three(bank[:, GATE_BANK + b, :], w["g_hi"][:, p, :], w["g_lo"][:, p, :],
                      x_hi, x_lo, True, True).then_inc(gate_ready, 1)
                if p >= LAG:
                    down(c, par, p - LAG)
                elif not is_first(c):
                    down(c - 1, 1 - par, PAIRS - LAG + p)
                for name in steps_at(c, p, 0):
                    step(name, c, par)

            for name in first_steps:
                step(name, -1, 1)
            on_chunks(pe, slot)
            for p in range(PAIRS - LAG, PAIRS):
                down(CHUNKS - 1, (CHUNKS - 1) % 2, p)
            for name in last_steps:
                step(name, CHUNKS, CHUNKS % 2)

        @block.scalar
        def _(act):
            def copy_y(c, par):
                after(act, down_done, PAIRS * c)
                if isinstance(c, int) and c == CHUNKS:
                    act.wait_ge(misc_ready, count("add", c - 1))
                act.activation(y_sb[:], bank[:, Y_BANK + 1 - par, :], ACT.Copy).then_inc(y_made, 1)

            def read(name, c, par):
                n = count(name, c)
                nxt = 1 - par
                if name == "turn_x":
                    after(act, misc_ready, n)
                    act.activation(x_t[:, nxt, 0, :], misc, ACT.Copy).then_inc(misc_half, 1)
                elif name == "turn_w":
                    after(act, misc_ready, n)
                    after(act, comb_stored, 16 * (c + 1))
                    act.activation(comb_t[:], misc[0:EXPERTS, :], ACT.Copy).then_inc(misc_read, 1)
                elif name == "turn_n":
                    after(act, misc_ready, n)
                    act.activation(x2_t[:], misc, ACT.Copy).then_inc(misc_read, 1)
                elif name in ("q", "k"):
                    hold(act, proj_stats_made, 3 * (c - 1) + "qkv".index(name) + 1)
                    act.activation(rows(qkv[name], c - 1).rearrange("p a b -> p (a b)"), misc,
                                   ACT.Copy).then_inc(misc_read, 1)
                elif name == "v":
                    after(act, proj_stats_made, 3 * (c - 1) + 3)
                    act.activation(v_t[:], misc, ACT.Copy).then_inc(misc_read, 1)
                elif name == "turn_v":
                    hold(act, misc_ready, n)
                    act.activation(rows(qkv["v"], c - 1).rearrange("p a b -> p (a b)"), misc,
                                   ACT.Copy).then_inc(misc_read, 1)

            def split_hi(g, p):
                after(act, hid_made, g + 1)
                after(act, down_done, g + 1 - HSPLIT)
                act.activation(hid_hi[:, p % HSPLIT, :], hid[:, p % 2, :], ACT.Copy).then_inc(hi_made, 1)

            def tanh_z(k):
                after(act, z_made, k + 1)
                act.activation(th[:], z[:], ACT.Tanh, scale=0.5).then_inc(th_made, 1)

            def slot(c, par, p):
                g = PAIRS * c + p
                for name in steps_at(c, p, 1):
                    read(name, c, par)
                if p == LAG and not is_first(c):
                    copy_y(c, par)
                if p == 6 and (not isinstance(c, int) or c < CHUNKS - 1):
                    tanh_z(c + 1)
                after(act, gate_ready, g + 1)
                gate_bank = bank[:, GATE_BANK + p % 2, :]
                act.activation(gate_bank, gate_bank, ACT.Silu).then_inc(silu_made, 1)
                if not (is_first(c) and p == 0):
                    split_hi(g - 1, (p - 1) % PAIRS)

            for name in first_steps:
                if name == "turn_w":
                    tanh_z(0)
                read(name, -1, 1)
            on_chunks(act, slot)
            split_hi(PAIRS * CHUNKS - 1, PAIRS - 1)
            copy_y(CHUNKS, CHUNKS % 2)
            for name in last_steps:
                read(name, CHUNKS, CHUNKS % 2)

        @block.vector
        def _(dve):
            def ln_stats(ln, chunk, k, also=None):
                if also is not None:
                    hold(dve, misc_read, also)
                x = rows(x_sb, chunk)
                for i in range(TILES):
                    last = dve.bn_stats(ln["stats"][:, i, :], x[:, i, :])
                last.then_inc(ln["stats_made"], 1)
                hold(dve, ln["stats_made"], k + 1)
                for i in range(TILES):
                    last = dve.bn_aggr(ln["mv"][:, i, :], ln["stats"][:, i, :])
                last.then_inc(ln["mv_made"], 1)

            def ln_apply(ln, chunk, k):
                hold(dve, ln["rstd_made"], k + 1)
                x = rows(x_sb, chunk)
                for i in range(TILES):
                    last = dve.tensor_scalar(ln["xn"][:, i, :], x[:, i, :], ln["mv"][:, i, 0:1],
                                             ln["rstd"][:, i, :], ALU.subtract, ALU.mult)
                last.then_inc(ln["xn_made"], 1)

            def pick(c):
                k = c + 1
                after(dve, misc_ready, count("route", c))
                dve.tensor_copy(logits[:].rearrange("p a b -> p (a b)"),
                                misc[:, 0:TILES * EXPERTS]).then_inc(misc_read, 1)
                hold(dve, misc_read, count("route", c))
                for i in range(TILES):
                    last = dve.max(top[:, i, :], logits[:, i, :])
                last.then_inc(top_made, 1)
                after(dve, top_made, k + 1)
                dve.tensor_tensor(z[:], logits[:], top[:, :, 0:1].to_broadcast([P, TILES, EXPERTS]),
                                  ALU.subtract).then_inc(z_made, 1)
                for i in range(TILES):
                    last = dve.match_replace(rest[:, i, :], top[:, i, :], logits[:, i, :], MASKED)
                last.then_inc(rest_made, 1)
                after(dve, rest_made, k + 1)
                dve.tensor_tensor(chosen[:], logits[:], rest[:], ALU.not_equal).then_inc(chosen_made, 1)

            def weigh(c):
                k = c + 1
                after(dve, th_made, k + 1)
                dve.tensor_scalar(den[:], th[:], -1.0, 1.0, ALU.mult, ALU.add).then_inc(den_made, 1)
                after(dve, chosen_made, k + 1)
                dve.scalar_tensor_tensor(out=num[:], in0=th[:], scalar=1.0, in1=chosen[:],
                                         op0=ALU.add, op1=ALU.mult).then_inc(num_made, 1)
                after(dve, den_made, k + 1)
                dve.reciprocal(den_inv[:], den[:]).then_inc(den_inv_made, 1)
                after(dve, num_made, k + 1)
                after(dve, den_inv_made, k + 1)
                dve.tensor_tensor(wt[:], num[:], den_inv[:], ALU.mult).then_inc(wt_made, 1)
                after(dve, wt_made, k + 1)
                dve.tensor_reduce(wsum[:], wt[:], AX_X, ALU.add).then_inc(wsum_made, 1)
                after(dve, wsum_made, k + 1)
                dve.reciprocal(winv[:], wsum[:]).then_inc(winv_made, 1)
                after(dve, winv_made, k + 1)
                dve.scalar_tensor_tensor(out=wn[:], in0=wt[:], scalar=0.5,
                                         in1=winv[:].to_broadcast([P, TILES, EXPERTS]),
                                         op0=ALU.mult, op1=ALU.mult).then_inc(wn_made, 1)

            def read(name, c, par):
                n = count(name, c)
                nxt = 1 - par
                if name == "add":
                    x = rows(x_sb, c - 1)
                    after(dve, misc_ready, n)
                    dve.tensor_tensor(x, misc.rearrange("p (a b) -> p a b", a=TILES), x,
                                      ALU.add).then_inc(misc_read, 1)
                elif name == "turn_x":
                    after(dve, misc_half, c + 2)
                    dve.tensor_tensor(x_t[:, nxt, 1, :], misc, x_t[:, nxt, 0, :].bitcast(F32),
                                      ALU.subtract).then_inc(misc_read, 1)
                elif name == "route":
                    pick(c)
                elif name in ("q", "k", "v"):
                    m = "qkv".index(name)
                    hold(dve, misc_ready, n)
                    at = c - 1 + CHUNKS * m
                    dst = w["proj_stats"][:, at, :] if isinstance(at, int) else w["proj_stats"][:, bass.ds(at, 1), :]
                    dve.bn_stats(dst, misc).then_inc(proj_stats_made, 1)

            def slot(c, par, p):
                g = PAIRS * c + p
                b = p % 2
                for name in steps_at(c, p, 1):
                    read(name, c, par)
                follows = not isinstance(c, int) or c < CHUNKS - 1
                if follows and p == 0:
                    ln_stats(ln_f, c + 1, c + 1)
                if follows and p == 2:
                    ln_apply(ln_f, c + 1, c + 1)
                if follows and p == 7:
                    weigh(c)
                if qkv and not is_first(c):
                    if p == 6:
                        ln_stats(ln_q, c - 1, c - 1, count("add", c))
                    if p == 8:
                        ln_apply(ln_q, c - 1, c - 1)
                if p % GROUP == 0:
                    q = p // GROUP
                    after(dve, share_in[q % 2], 32 * (2 * c + q // 2 + 1))
                after(dve, up_ready, g + 1)
                after(dve, hid_made, g - 1)
                dve.tensor_tensor(scaled[:, b, :], bank[:, UP_BANK + b, :],
                                  share[:, p // GROUP % 2, p % GROUP, :], ALU.mult).then_inc(scaled_made, 1)
                after(dve, scaled_made, g + 1)
                after(dve, silu_made, g + 1)
                after(dve, lo_made, g - 1)
                dve.tensor_tensor(hid[:, b, :], bank[:, GATE_BANK + b, :], scaled[:, b, :],
                                  ALU.mult).then_inc(hid_made, 1)

            ln_stats(ln_f, 0, 0)
            ln_apply(ln_f, 0, 0)
            for name in first_steps:
                read(name, -1, 1)
            weigh(-1)
            on_chunks(dve, slot)
            read("add", CHUNKS, 0)
            if qkv:
                ln_stats(ln_q, CHUNKS - 1, CHUNKS - 1, count("add", CHUNKS))
                ln_apply(ln_q, CHUNKS - 1, CHUNKS - 1)
                for name in ("q", "k", "v"):
                    read(name, CHUNKS, 0)

        @block.gpsimd
        def _(pool):
            def rstd(ln, k):
                after(pool, ln["mv_made"], k + 1)
                pool.tensor_tensor(ln["ve"][:], ln["mv"][:, :, 1:2], w["eps"][:], ALU.add).then_inc(ln["ve_made"], 1)
                after(pool, ln["ve_made"], k + 1)
                pool.tensor_tensor(ln["rstd"][:], ln["ve"][:], w["neg_half"][:], ALU.pow).then_inc(ln["rstd_made"], 1)

            def slot(c, par, p):
                g = PAIRS * c + p
                follows = not isinstance(c, int) or c < CHUNKS - 1
                if follows and p == 0:
                    rstd(ln_f, c + 1)
                if qkv and not is_first(c) and p == 6:
                    rstd(ln_q, c - 1)
                after(pool, hi_made, g + 1)
                pool.tensor_tensor(hid_lo[:, p % HSPLIT, :], hid[:, p % 2, :],
                                   hid_hi[:, p % HSPLIT, :].bitcast(F32), ALU.subtract).then_inc(lo_made, 1)

            rstd(ln_f, 0)
            on_chunks(pool, slot)
            if qkv:
                rstd(ln_q, CHUNKS - 1)

        @block.sync
        def _(sp):
            def send_comb(k, par):
                hold(sp, misc_read, count("turn_w", k - 1))
                sp.dma_start(comb_d[par], comb_t[:]).then_inc(comb_stored, 16)

            def spread(c, par, q):
                if q == 0:
                    hold(sp, comb_stored, 16 * (c + 1))
                hold(sp, scaled_made, PAIRS * c + GROUP * (q - 1))
                for half in range(2):
                    src = comb_d[par].rearrange("(n two) t -> two n t", two=2)[half, GROUP * q:GROUP * q + GROUP, :]
                    sp.dma_start(share[half * EDIM:half * EDIM + EDIM, q % 2, :, :],
                                 src.partition_broadcast(EDIM)).then_inc(share_in[q % 2], 16)

            def store(c):
                hold(sp, misc_read, count("add", c))
                dst = out[c - 1] if isinstance(c, int) else out[bass.ds(c - 1, 1)].rearrange("a t h -> (a t) h")
                sp.dma_start(dst.rearrange("(n p) h -> p n h", p=P), rows(x_sb, c - 1)).then_inc(stored, 16)

            def chunk(c, par):
                spread(c, par, 2)
                if out is not None and not is_first(c):
                    store(c)
                spread(c, par, 3)
                if not isinstance(c, int) or c < CHUNKS - 1:
                    send_comb(c + 1, 1 - par)
                    spread(c + 1, 1 - par, 0)
                    spread(c + 1, 1 - par, 1)

            send_comb(0, 0)
            spread(0, 0, 0)
            spread(0, 0, 1)
            chunk(0, 0)
            with sp.Fori(0, (CHUNKS - 2) // UNROLL) as k:
                for u in range(1, 1 + UNROLL):
                    chunk(k * UNROLL + u, u % 2)
            chunk(CHUNKS - 1, (CHUNKS - 1) % 2)
            if out is not None:
                store(CHUNKS)
                sp.wait_ge(stored, 16 * CHUNKS)


def attention_block(nc, w, x_sb, bank, qkv):
    with ExitStack() as ctx:
        def sb(name, shape, dt=F32):
            return ctx.enter_context(nc.sbuf_tensor(name, shape, dt))

        def sem(name):
            return ctx.enter_context(nc.semaphore(name))

        bn_mv = sb("bn_mv", [P, 3, 2])
        bn_ve = sb("bn_ve", [P, 3, 1])
        bn_rstd = sb("bn_rstd", [P, 3, 1])
        bn_scale = sb("bn_scale", [P, 3])
        bn_mean = sb("bn_mean", [P, 3])
        bn_shift = sb("bn_shift", [P, 3])
        q_scale = sb("q_scale", [P, 1])
        q_shift = sb("q_shift", [P, 1])
        v_shift = sb("v_shift", [P, P])
        out_v = sb("out_v", [P, P])
        shift_row = sb("shift_row", [P, P])
        q_n = sb("q_n", [P, CHUNK])
        k_n = sb("k_n", [P, CHUNK])
        v_n = sb("v_n", [P, TILES, P])
        probs = sb("probs", [P, TILES, CHUNK])
        probs_t = sb("probs_t", [P, TILES, CHUNK])
        low = sb("low", [P, TILES])
        psum_row = sb("psum_row", [P, TILES])
        inv_row = sb("inv_row", [P, TILES])
        y_sb = sb("y_att", [P, CHUNK])

        bn_step = sem("bn_step")
        bn_ve_made = sem("bn_ve_made")
        bn_rstd_made = sem("bn_rstd_made")
        shift_ready = sem("shift_ready")
        shift_made = sem("shift_made")
        shift_added = sem("shift_added")
        q_made = sem("q_made")
        k_made = sem("k_made")
        v_made = sem("v_made")
        s_ready = sem("s_ready")
        low_made = sem("low_made")
        exp_made = sem("exp_made")
        t_ready = sem("t_ready")
        even_made = sem("even_made")
        odd_made = sem("odd_made")
        y_ready = sem("y_ready")
        y_made = sem("y_made")
        o_ready = sem("o_ready")
        inv_made = sem("inv_made")
        x_done = sem("x_done")
        block = ctx.enter_context(nc.Block())

        T_BANK, Y_BANK, O_BANK = 4, 6, 7
        y_bank = bank[:, Y_BANK, :]
        o_bank = bank[:, O_BANK, :]
        SCALE = float(P) ** -0.5

        def on_rows(eng, part):
            part(-1)
            part(0)
            with eng.Fori(1, CHUNKS - 1) as b:
                part(b)
            part(CHUNKS - 1)
            part(CHUNKS)

        def runs(b):
            return not isinstance(b, int) or 0 <= b < CHUNKS

        def scored(b):
            return not isinstance(b, int) or b + 1 < CHUNKS

        def has_last(b):
            return not isinstance(b, int) or b >= 1

        def flat(t, b):
            return rows(t, b).rearrange("p a b -> p (a b)")

        @block.tensor
        def _(pe):
            pe.wait_ge(bn_step, 9)
            pe.matmul(o_bank[:, 0:P], v_shift[:], w["out_t"][:], start=True, stop=True).then_inc(shift_ready, 1)

            def turn(b, j):
                if j == 0:
                    after(pe, exp_made, TILES * b + TILES)
                after(pe, (even_made, odd_made)[j % 2], 2 * b + j // 2)
                for i in range(j, TILES):
                    last = pe.transpose(bank[:, T_BANK + j % 2, i * P:i * P + P], probs[:, i, j * P:j * P + P],
                                        w["ident"][:])
                last.then_inc(t_ready, 1)

            def scores(b, i):
                if i == 0:
                    after(pe, q_made, b + 1)
                    after(pe, k_made, b + 1)
                after(pe, exp_made, TILES * (b - 1) + i + 1)
                n = i * P + P
                if i:
                    pe.matmul(bank[:, i, 0:i * P], q_n[:, i * P:n], k_n[:, 0:i * P], start=True, stop=True)
                pe.matmul(bank[:, i, i * P:n], q_n[:, i * P:n], k_n[:, i * P:n], start=True, stop=False)
                pe.matmul(bank[:, i, i * P:n], w["ident_b"][:], w["causal_b"][:], start=False,
                          stop=True).then_inc(s_ready, 1)

            def part(b):
                if runs(b):
                    turn(b, 0)
                    turn(b, 1)
                if has_last(b):
                    after(pe, y_made, b)
                    after(pe, x_done, b - 1)
                    for i in range(TILES):
                        last = pe.matmul(o_bank[:, i * P:i * P + P], y_sb[:, i * P:i * P + P], out_v[:],
                                         start=True, stop=True)
                    last.then_inc(o_ready, 1)
                if scored(b):
                    scores(b + 1, 0)
                    scores(b + 1, 1)
                if runs(b):
                    turn(b, 2)
                    turn(b, 3)
                if scored(b):
                    scores(b + 1, 2)
                    scores(b + 1, 3)
                if runs(b):
                    after(pe, v_made, b + 1)
                    after(pe, y_made, b)
                    for j in range(TILES):
                        after(pe, (even_made, odd_made)[j % 2], 2 * b + j // 2 + 1)
                        last = pe.matmul(y_bank[:, j * P:CHUNK], v_n[:, j, :], probs_t[:, j, j * P:CHUNK],
                                         start=(j == 0), stop=True, skip_group_check=(j > 0))
                    last.then_inc(y_ready, 1)

            pe.wait_ge(shift_made, 1)
            on_rows(pe, part)

        @block.scalar
        def _(act):
            act.wait_ge(shift_ready, 1)
            act.activation(shift_row[:], o_bank[:, 0:P], ACT.Copy).then_inc(shift_made, 1)
            act.wait_ge(bn_step, 9)

            def exps(b, i):
                after(act, low_made, TILES * b + i + 1)
                after(act, t_ready, TILES * (b - 1) + i + 1)
                after(act, inv_made, b)
                n = i * P + P
                act.activation(probs[:, i, 0:n], bank[:, i, 0:n], ACT.Exp, scale=-1.0, bias=low[:, i:i + 1],
                               accum_out=psum_row[:, i:i + 1]).then_inc(exp_made, 1)

            def odd(b, j):
                after(act, t_ready, TILES * b + j + 1)
                after(act, y_ready, b)
                act.activation(probs_t[:, j, j * P:CHUNK], bank[:, T_BANK + 1, j * P:CHUNK],
                               ACT.Copy).then_inc(odd_made, 1)

            def part(b):
                if scored(b):
                    hold(act, s_ready, TILES * (b + 1))
                    act.activation(q_n[:], flat(qkv["q"], b + 1), ACT.Identity, scale=q_scale[:],
                                   bias=q_shift[:]).then_inc(q_made, 1)
                if runs(b):
                    odd(b, 1)
                if scored(b):
                    exps(b + 1, 0)
                    exps(b + 1, 1)
                if runs(b):
                    odd(b, 3)
                if scored(b):
                    exps(b + 1, 2)
                    exps(b + 1, 3)
                if runs(b):
                    after(act, y_ready, b + 1)
                    after(act, o_ready, b)
                    act.activation(y_sb[:], y_bank, ACT.Copy).then_inc(y_made, 1)

            on_rows(act, part)

        @block.vector
        def _(dve):
            for m in range(3):
                last = dve.bn_aggr(bn_mv[:, m, :], w["proj_stats"][:, m * CHUNKS:(m + 1) * CHUNKS, :])
            last.then_inc(bn_step, 1)
            dve.wait_ge(bn_rstd_made, 1)
            col = lambda t: t[:].rearrange("p (a b) -> p a b", b=1)
            dve.tensor_tensor(col(bn_scale), w["gamma_beta"][:, 0:3].rearrange("p (a b) -> p a b", b=1), bn_rstd[:], ALU.mult).then_inc(bn_step, 1)
            dve.wait_ge(bn_step, 2)
            dve.tensor_tensor(col(bn_mean), bn_mv[:, :, 0:1], col(bn_scale), ALU.mult).then_inc(bn_step, 1)
            dve.wait_ge(bn_step, 3)
            dve.tensor_tensor(bn_shift[:], w["gamma_beta"][:, 3:6], bn_mean[:], ALU.subtract).then_inc(bn_step, 1)
            dve.wait_ge(bn_step, 4)
            dve.tensor_scalar(q_scale[:], bn_scale[:, 0:1], -SCALE, None, ALU.mult).then_inc(bn_step, 1)
            dve.tensor_scalar(q_shift[:], bn_shift[:, 0:1], -SCALE, None, ALU.mult).then_inc(bn_step, 1)
            dve.tensor_scalar(out_v[:], w["out_t"][:], bn_scale[:, 2:3], None, ALU.mult).then_inc(bn_step, 1)
            dve.tensor_copy(v_shift[:], bn_shift[:, 2:3].to_broadcast([P, P])).then_inc(bn_step, 1)
            dve.memset(low[:], 0.0).then_inc(bn_step, 1)
            dve.wait_ge(bn_step, 9)

            def even(b, j):
                after(dve, t_ready, TILES * b + j + 1)
                after(dve, y_ready, b)
                dve.tensor_copy(probs_t[:, j, j * P:CHUNK], bank[:, T_BANK, j * P:CHUNK]).then_inc(even_made, 1)

            def lows(b, i):
                after(dve, s_ready, TILES * b + i + 1)
                after(dve, exp_made, TILES * (b - 1) + i + 1)
                dve.tensor_reduce(low[:, i:i + 1], bank[:, i, 0:i * P + P], AX_X, ALU.min).then_inc(low_made, 1)

            def part(b):
                if scored(b):
                    after(dve, s_ready, TILES * (b + 1))
                    dve.tensor_scalar(k_n[:], flat(qkv["k"], b + 1), bn_scale[:, 1:2], bn_shift[:, 1:2],
                                      ALU.mult, ALU.add).then_inc(k_made, 1)
                if runs(b):
                    even(b, 0)
                if has_last(b):
                    dve.wait_ge(shift_added, 1)
                    hold(dve, o_ready, b)
                    hold(dve, inv_made, b)
                    x = rows(x_sb, b - 1)
                    for i in range(TILES):
                        last = dve.scalar_tensor_tensor(out=x[:, i, :], in0=o_bank[:, i * P:i * P + P],
                                                        scalar=inv_row[:, i:i + 1], in1=x[:, i, :],
                                                        op0=ALU.mult, op1=ALU.add)
                    last.then_inc(x_done, 1)
                if runs(b):
                    after(dve, exp_made, TILES * b + TILES)
                    after(dve, x_done, b)
                    dve.reciprocal(inv_row[:], psum_row[:]).then_inc(inv_made, 1)
                if scored(b):
                    lows(b + 1, 0)
                    lows(b + 1, 1)
                if runs(b):
                    even(b, 2)
                if scored(b):
                    lows(b + 1, 2)
                    lows(b + 1, 3)

            on_rows(dve, part)

        @block.gpsimd
        def _(pool):
            pool.wait_ge(bn_step, 1)
            pool.tensor_tensor(bn_ve[:], bn_mv[:, :, 1:2], w["eps"][:, 0:3, :], ALU.add).then_inc(bn_ve_made, 1)
            pool.wait_ge(bn_ve_made, 1)
            pool.tensor_tensor(bn_rstd[:], bn_ve[:], w["neg_half"][:, 0:3, :], ALU.pow).then_inc(bn_rstd_made, 1)

            def copy_v(b):
                hold(pool, y_ready, b)
                pool.tensor_copy(v_n[:], rows(qkv["v"], b)).then_inc(v_made, 1)

            copy_v(0)
            pool.wait_ge(shift_made, 1)
            pool.tensor_tensor(x_sb[:], x_sb[:], shift_row[:].rearrange("p (a b) -> p a b", a=1)
                               .to_broadcast([P, TILES * CHUNKS, P]), ALU.add).then_inc(shift_added, 1)
            with pool.Fori(1, CHUNKS) as b:
                copy_v(b)


def build(nc, x, W_attn, W_proj, lora_attn_A, lora_attn_B, lora_proj_A, lora_proj_B, gamma, beta, gate, gate_up,
          down, out):
    d = {"x": x, "W_attn": W_attn, "W_proj": W_proj, "lora_attn_A": lora_attn_A, "lora_attn_B": lora_attn_B,
         "lora_proj_A": lora_proj_A, "lora_proj_B": lora_proj_B, "gamma": gamma, "beta": beta, "gate": gate,
         "gate_up": gate_up, "down": down}
    with ExitStack() as ctx:
        def sb(name, shape, dt=F32):
            return ctx.enter_context(nc.sbuf_tensor(name, shape, dt))

        bank = ctx.enter_context(nc.psum_tensor("bank", [P, 8, CHUNK], F32))
        x_sb = sb("x_sb", [P, CHUNKS * TILES, P])
        w = {n: sb(n, [P, PAIRS, P], F32R) for n in ("g_hi", "g_lo", "u_hi", "u_lo", "d_hi", "d_lo")}
        w |= {n: sb(n, [P, EXPERTS], F32R) for n in ("r_hi", "r_lo")}
        w |= {"qkv_t": sb("qkv_t", [P, 3 * P]), "out_t": sb("out_t", [P, P]), "ident": sb("ident", [P, P]),
              "causal": sb("causal", [P, P]), "ident_b": sb("ident_b", [P, P], mybir.dt.bfloat16),
              "causal_b": sb("causal_b", [P, P], mybir.dt.bfloat16),
              "gamma_beta": sb("gamma_beta", [P, 6]),
              "eps": sb("eps", [P, TILES, 1]), "neg_half": sb("neg_half", [P, TILES, 1]),
              "proj_stats": sb("proj_stats", [P, 3 * CHUNKS, 6])}
        setup_block(nc, d, w, x_sb, bank)
        with ExitStack() as inner:
            qkv = {n: inner.enter_context(nc.sbuf_tensor(f"{n}_all", [P, CHUNKS * TILES, P], F32)) for n in "qkv"}
            ffn_block(nc, w, x_sb, bank, qkv, None)
            attention_block(nc, w, x_sb, bank, qkv)
        ffn_block(nc, w, x_sb, bank, None, out)


_INS = ["L0_attn_x", "L0_attn_W_attn", "L0_attn_W_proj", "L0_attn_lora_attn_A", "L0_attn_lora_attn_B",
        "L0_attn_lora_proj_A", "L0_attn_lora_proj_B", "L0_attn_bn_gamma", "L0_attn_bn_beta",
        "L0_ffn_gate_w", "L0_ffn_gate_up_w", "L0_ffn_down_w"]


def kernel(**inputs):
    import concourse.bacc as bacc
    from concourse.bass_utils import run_bass_kernel_spmd

    nc = bacc.Bacc("TRN2", target_bir_lowering=False, num_devices=1)
    arrays, args = {}, []
    for name in _INS:
        a = np.ascontiguousarray(inputs[name])
        arrays[name] = a
        args.append(nc.dram_tensor(name, a.shape, mybir.dt.from_np(a.dtype), kind="ExternalInput").ap())
    shape = arrays["L0_attn_x"].shape
    args.append(nc.dram_tensor("y_out", shape, F32, kind="ExternalOutput").ap())
    build(nc, *args)
    r = run_bass_kernel_spmd(nc, [arrays], core_ids=[0])
    return r.results[0]["y_out"]
```

```python
from contextlib import ExitStack

import numpy as np

import concourse.bass as bass
from concourse import mybir

F32 = mybir.dt.float32
F32R = mybir.dt.float32r
ALU = mybir.AluOpType
ACT = mybir.ActivationFunctionType
AX_X = mybir.AxisListType.X

P = 128
TILES = 4
CHUNK = TILES * P
CHUNKS = 8
EXPERTS = 32
EDIM = 64
PAIRS = EXPERTS // 2
TOPK = 8
EPS = 1e-5
MASKED = -1e30
LAG = 3
GROUP = 4
HSPLIT = 4
UNROLL = 2


class Phase:
    def __init__(self, tensor, scalar, vector, gpsimd, sync):
        self.tensor, self.scalar, self.vector, self.gpsimd, self.sync = tensor, scalar, vector, gpsimd, sync


class Parts:
    def __init__(self, ahead, main):
        self.ahead, self.main = ahead, main


def after(eng, sem, value):
    if not isinstance(value, int) or value > 0:
        eng.wait_ge(sem, value)


def hold(eng, sem, value):
    if isinstance(value, int):
        after(eng, sem, value)
    else:
        eng.wait_ge(sem, value)
        eng.nop(nofuse=True)


def rows(x_sb, c):
    return x_sb[:, TILES * c:TILES * c + TILES, :] if isinstance(c, int) else x_sb[:, bass.ds(TILES * c, TILES), :]


def setup_phase(ctx, nc, d, w, x_sb, bank, qkv):
    def sem(name):
        return ctx.enter_context(nc.semaphore(name))

    gu_nat = qkv["q"][:]
    flat_k = qkv["k"][:].rearrange("p a b -> p (a b)")
    dn_nat = flat_k[:, 0:EXPERTS * EDIM]
    attn_nat = qkv["k"][:, 16:19, :]
    proj_nat = qkv["k"][:, 19, :]
    gate_nat = qkv["k"][0:EXPERTS, 20, :]
    la_a = qkv["k"][:, 21, 0:EDIM]
    lp_a = qkv["k"][:, 21, EDIM:2 * EDIM]
    la_b = flat_k[0:EDIM, 22 * P:25 * P]
    lp_b = qkv["k"][0:EDIM, 25, :]
    bn_nat = qkv["k"][0:6, 26, :]
    la_at = qkv["k"][0:EDIM, 27, :]
    lp_at = qkv["k"][0:EDIM, 28, :]
    projm_t = qkv["k"][:, 29, :]
    delta = qkv["v"][:, 0:3, :].rearrange("p a b -> p (a b)")
    causal = qkv["v"][:, 3, :]

    GUS = 8
    DNS = 4
    gu_in = [sem(f"gu_in{i}") for i in range(GUS)]
    dn_in = [sem(f"dn_in{i}") for i in range(DNS)]
    gate_in = sem("gate_in")
    small_in = sem("small_in")
    x_in = [sem(f"x_in{i}") for i in range(3)]
    const_step = sem("const_step")
    turned = sem("turned")
    copied = sem("copied")
    passed = sem("passed")

    steps = {"gate": -1, "gu0": -1, "gu1": 0, "dn0": 1, "gu2": 2, "lora": 3, "gu3": 4, "dn1": 5, "gu4": 6,
             "attn": 7, "gu5": 8, "dn2": 9, "gu6": 10, "delta": 11, "gu7": 12, "dn3": 13, "projm": 14,
             "comb": 14}
    number = {name: n + 1 for n, name in enumerate(steps)}
    b = bank[:, 6, :]

    def sync(sp):
        def gu(q):
            sp.dma_start(gu_nat[:, 4 * q:4 * q + 4, :],
                         d["gate_up"][4 * q:4 * q + 4].rearrange("e (i j) h -> (e i) j h", j=4)).then_inc(gu_in[q], 16)

        def dn(q):
            n = EXPERTS // DNS
            sp.dma_start(dn_nat[:, q * n * EDIM:(q + 1) * n * EDIM].rearrange("h (e k) -> h e k", e=n),
                         d["down"][n * q:n * q + n].rearrange("e h k -> h e k")).then_inc(dn_in[q], 16)

        sp.dma_start(x_sb[:, 0:TILES, :], d["x"][0].rearrange("(n p) h -> p n h", p=P)).then_inc(x_in[0], 16)
        gu(0)
        gu(1)
        sp.dma_start(x_sb[:, TILES:2 * TILES, :], d["x"][1].rearrange("(n p) h -> p n h", p=P)).then_inc(x_in[1], 16)
        dn(0)
        for q in range(2, 4):
            gu(q)
        dn(1)
        gu(4)
        gu(5)
        dn(2)
        gu(6)
        gu(7)
        dn(3)
        sp.dma_start(x_sb[:, 2 * TILES:, :].rearrange("p (c n) h -> p c n h", n=TILES),
                     d["x"][2:].rearrange("c (n p) h -> p c n h", p=P)).then_inc(x_in[2], 16)

    def loads(act):
        act.dma_start(gate_nat, d["gate"]).then_inc(gate_in, 16)
        for dst, src in ((attn_nat, d["W_attn"].rearrange("(m p) c -> p m c", p=P)), (proj_nat, d["W_proj"]),
                         (la_a, d["lora_attn_A"]), (lp_a, d["lora_proj_A"]), (la_b, d["lora_attn_B"]),
                         (lp_b, d["lora_proj_B"]), (bn_nat[0:3, :], d["gamma"].rearrange("(m p) -> m p", p=P)),
                         (bn_nat[3:6, :], d["beta"].rearrange("(m p) -> m p", p=P))):
            act.dma_start(dst, src).then_inc(small_in, 16)

    def halves(q):
        t = b.rearrange("h (j e f i) -> h f e i j", j=4, e=4, f=2)
        s = slice(2 * q, 2 * q + 2)
        for f, (hi, lo) in enumerate((("g_hi", "g_lo"), ("u_hi", "u_lo"))):
            yield t[:, f], *(w[n][:, s, :].rearrange("h a (b i j) -> h (a b) i j", b=2, j=4) for n in (hi, lo))

    def scalar(act, name):
        act.wait_ge(turned, number[name])
        if name[:2] == "gu":
            for t, hi, lo in halves(int(name[2])):
                i = act.activation(hi, t, ACT.Copy)
        elif name[:2] == "dn":
            q = int(name[2])
            i = act.activation(w["d_hi"][:, 4 * q:4 * q + 4, :].rearrange("p a b -> p (a b)"), b, ACT.Copy)
        elif name == "gate":
            i = act.activation(w["r_hi"][:], b[:, 0:EXPERTS], ACT.Copy)
        elif name == "lora":
            act.activation(la_at, b[0:EDIM, 0:P], ACT.Copy)
            i = act.activation(lp_at, b[0:EDIM, P:2 * P], ACT.Copy)
        elif name == "attn":
            act.activation(w["gamma_beta"][:], b[:, 3 * P:3 * P + 6], ACT.Copy)
            i = act.activation(w["qkv_t"][:], b[:, 0:3 * P], ACT.Copy)
        elif name == "delta":
            i = act.activation(delta, b[:, 0:3 * P], ACT.Copy)
        elif name == "projm":
            i = act.activation(projm_t, b[:, 0:P], ACT.Copy)
        elif name == "comb":
            i = act.activation(w["out_t"][:], b[:, 0:P], ACT.Copy)
        i.then_inc(copied, 1)

    def vector(dve, name):
        dve.wait_ge(copied, number[name])
        if name[:2] == "gu":
            for t, hi, lo in halves(int(name[2])):
                i = dve.tensor_tensor(lo, t, hi.bitcast(F32), ALU.subtract)
        elif name[:2] == "dn":
            q = int(name[2])
            s = slice(4 * q, 4 * q + 4)
            i = dve.tensor_tensor(w["d_lo"][:, s, :].rearrange("p a b -> p (a b)"), b,
                                  w["d_hi"][:, s, :].bitcast(F32).rearrange("p a b -> p (a b)"), ALU.subtract)
        elif name == "gate":
            i = dve.tensor_tensor(w["r_lo"][:], b[:, 0:EXPERTS], w["r_hi"][:].bitcast(F32), ALU.subtract)
        elif name == "delta":
            qkv_t = w["qkv_t"][:].rearrange("c (r j) -> c r j", j=3)
            i = dve.tensor_tensor(qkv_t, delta.rearrange("c (j r) -> c r j", j=3), qkv_t, ALU.add)
        else:
            i = dve.memset(w["nothing"][:], 0.0)
        i.then_inc(passed, 1)

    def gpsimd(pool):
        pool.memset(w["ident"][:], 0.0).then_inc(const_step, 1)
        pool.wait_ge(const_step, 1)
        pool.affine_select(out=w["ident"][:], in_=w["ident"][:], compare_op=ALU.not_equal, fill=1.0, base=0,
                           pattern=[[-1, P]], channel_multiplier=1).then_inc(const_step, 1)
        pool.memset(w["neg_half"][:], -0.5).then_inc(const_step, 1)
        pool.memset(w["eps"][:], EPS).then_inc(const_step, 1)
        pool.memset(causal, 0.0).then_inc(const_step, 1)
        pool.wait_ge(const_step, 5)
        pool.affine_select(out=causal, in_=causal, compare_op=ALU.is_ge, fill=-MASKED, base=0,
                           pattern=[[-1, P]], channel_multiplier=1).then_inc(const_step, 1)
        pool.wait_ge(const_step, 6)
        pool.tensor_copy(w["causal_b"][:], causal).then_inc(const_step, 1)
        pool.tensor_copy(w["ident_b"][:], w["ident"][:]).then_inc(const_step, 1)

    def tensor(pe, name):
        ident = w["ident"]
        if name == "gate":
            pe.wait_ge(const_step, 2)
            pe.wait_ge(gate_in, 16)
        after(pe, passed, number[name] - 1)
        if name[:2] == "gu":
            q = int(name[2])
            pe.wait_ge(gu_in[q], 16)
            for j in range(4):
                i = pe.transpose(b[:, j * P:j * P + P], gu_nat[:, 4 * q + j, :], ident[:])
        elif name[:2] == "dn":
            q = int(name[2])
            pe.wait_ge(dn_in[q], 16)
            for e in range(4):
                n = 4 * q + e
                i = pe.transpose(b[:, e * P:e * P + P], dn_nat[:, n * P:n * P + P], ident[:])
        elif name == "gate":
            i = pe.transpose(b[:, 0:EXPERTS], gate_nat, ident[0:EXPERTS, 0:EXPERTS])
        elif name == "lora":
            pe.wait_ge(small_in, 16 * 8)
            pe.transpose(b[0:EDIM, 0:P], la_a, ident[:])
            i = pe.transpose(b[0:EDIM, P:2 * P], lp_a, ident[:])
        elif name == "attn":
            for m in range(3):
                pe.transpose(b[:, m * P:m * P + P], attn_nat[:, m, :], ident[:])
            i = pe.transpose(b[:, 3 * P:3 * P + 6], bn_nat, ident[0:6, 0:6])
        elif name == "delta":
            for j in range(3):
                i = pe.matmul(b[:, j * P:j * P + P], la_b[:, j * P:j * P + P], la_at, start=True, stop=True)
        elif name == "projm":
            pe.matmul(b[:, 0:P], proj_nat, ident[:], start=True, stop=False)
            i = pe.matmul(b[:, 0:P], lp_b, lp_at, start=False, stop=True)
        elif name == "comb":
            i = pe.matmul(b[:, 0:P], proj_nat, projm_t, start=True, stop=True)
        i.then_inc(turned, 1)

    setup = Phase(tensor, scalar, vector, gpsimd, sync)
    setup.steps, setup.loads, setup.x_in, setup.const_step = steps, loads, x_in, const_step
    return setup


def ffn_buffers(ctx, nc):
    def sb(name, shape, dt=F32):
        return ctx.enter_context(nc.sbuf_tensor(name, shape, dt))

    def ln_set(name):
        return {"stats": sb(f"{name}_stats", [P, TILES, 6]), "mv": sb(f"{name}_mv", [P, TILES, 2]),
                "ve": sb(f"{name}_ve", [P, TILES, 1]), "rstd": sb(f"{name}_rstd", [P, TILES, 1]),
                "shift": sb(f"{name}_shift", [P, TILES, 1]),
                "xn": sb(f"{name}_xn", [P, TILES, P])}

    small = {n: sb(n, [P, TILES, EXPERTS]) for n in
             ("logits", "rest", "z", "chosen", "th", "den", "den_inv", "num", "wt", "wn")}
    return dict(
        ln_f=ln_set("lnf"), ln_q=ln_set("lnq"),
        x_t=sb("x_t", [P, 2, 2, CHUNK], F32R),
        comb_t=sb("comb_t", [EXPERTS, CHUNK]),
        share=sb("share", [P, 2, GROUP, CHUNK]),
        scaled=sb("scaled", [P, 2, CHUNK]), hid=sb("hid", [P, 2, CHUNK]),
        hid_hi=sb("hid_hi", [P, HSPLIT, CHUNK], F32R), hid_lo=sb("hid_lo", [P, HSPLIT, CHUNK], F32R),
        y_sb=sb("y_sb", [P, CHUNK]), top=sb("top", [P, TILES, TOPK]),
        wsum=sb("wsum", [P, TILES, 1]), winv=sb("winv", [P, TILES, 1]), **small)


def ffn_phase(ctx, nc, tag, w, x_sb, bank, buf, qkv=None, setup=None, final=None, out=None):
    def sem(name):
        return ctx.enter_context(nc.semaphore(f"{name}_{tag}"))

    def ln_sems(name):
        return {n: sem(f"{name}_{n}") for n in ("stats_made", "mv_made", "ve_made", "rstd_made",
                                                "shift_made", "xn_made")}

    ln_f = buf["ln_f"] | ln_sems("lnf")
    ln_q = buf["ln_q"] | ln_sems("lnq") if qkv else None
    x_t, comb_t, share, scaled, hid = buf["x_t"], buf["comb_t"], buf["share"], buf["scaled"], buf["hid"]
    hid_hi, hid_lo, y_sb, top, wsum, winv = buf["hid_hi"], buf["hid_lo"], buf["y_sb"], buf["top"], buf["wsum"], buf["winv"]
    logits, rest, z, chosen, th = buf["logits"], buf["rest"], buf["z"], buf["chosen"], buf["th"]
    den, den_inv, num, wt, wn = buf["den"], buf["den_inv"], buf["num"], buf["wt"], buf["wn"]
    if qkv:
        x2_t, v_t = qkv["x2_t"], qkv["v_t"]
    comb_d = nc.dram_tensor(f"comb_{tag}", [2, EXPERTS, CHUNK], F32, kind="Internal").ap()

    gate_ready = sem("gate_ready")
    up_ready = sem("up_ready")
    silu_made = sem("silu_made")
    scaled_made = sem("scaled_made")
    hid_made = sem("hid_made")
    comb_stored = sem("comb_stored")
    share_in = [sem(f"share_in{i}") for i in range(2)]
    hi_made = sem("hi_made")
    lo_made = sem("lo_made")
    down_done = sem("down_done")
    y_made = sem("y_made")
    misc_ready = sem("misc_ready")
    misc_read = sem("misc_read")
    misc_half = sem("misc_half")
    top_made = sem("top_made")
    rest_made = sem("rest_made")
    z_made = sem("z_made")
    chosen_made = sem("chosen_made")
    th_made = sem("th_made")
    den_made = sem("den_made")
    den_inv_made = sem("den_inv_made")
    num_made = sem("num_made")
    wt_made = sem("wt_made")
    wsum_made = sem("wsum_made")
    winv_made = sem("winv_made")
    wn_made = sem("wn_made")
    proj_stats_made = sem("proj_stats_made")
    stored = sem("stored")

    GATE_BANK, UP_BANK, Y_BANK, MISC_BANK = 0, 2, 4, 7
    y_bank = bank[:, Y_BANK, :]
    misc = bank[:, MISC_BANK, :]

    NEXT, PREV = 1, -1
    STEPS = [("add", 3, PREV), ("turn_x", 4, NEXT), ("route", 5, NEXT), ("turn_w", 11, NEXT)]
    STEPS += [("turn_n", 12, PREV), ("q", 13, PREV), ("k", 13, PREV), ("v", 13, PREV),
              ("turn_v", 14, PREV)] if qkv else []
    PROJ_BANK = {"q": MISC_BANK, "k": 6, "v": 5}
    N_NEXT = sum(s[2] == NEXT for s in STEPS)
    N_PREV = len(STEPS) - N_NEXT

    def there(step, c):
        if not isinstance(c, int):
            return True
        return c >= 1 if step[2] == PREV else c <= CHUNKS - 2

    def before(c):
        if isinstance(c, int) and c < 1:
            return 0 if c < 0 else N_NEXT
        if isinstance(c, int) and c == CHUNKS:
            return before(c - 1) + N_PREV
        return 2 * N_NEXT + (c - 1) * (N_NEXT + N_PREV)

    def count(name, c):
        return before(c) + ([s[0] for s in STEPS if there(s, c)].index(name) + 1)

    def on_chunks(eng, slot):
        for p in range(PAIRS):
            slot(0, 0, p)
        with eng.Fori(0, (CHUNKS - 2) // UNROLL) as k:
            for u in range(1, 1 + UNROLL):
                for p in range(PAIRS):
                    slot(k * UNROLL + u, u % 2, p)
        for p in range(PAIRS):
            slot(CHUNKS - 1, (CHUNKS - 1) % 2, p)

    def steps_at(c, p, late):
        return [s[0] for s in STEPS if s[1] == p - late and there(s, c)]

    SETUP = setup.steps if setup else {}
    last_steps = [s[0] for s in STEPS if s[2] == PREV]

    def setup_at(c, p):
        return [n for n, at in SETUP.items() if at == p >= 0] if is_first(c) else []

    def is_first(c):
        return isinstance(c, int) and c == 0

    def tensor(pe):
        ident = w["ident"]

        def three(dst, hi, lo, x_hi, x_lo, start, stop):
            pe.matmul(dst, hi, x_hi, start=start, stop=False)
            pe.matmul(dst, hi, x_lo, start=False, stop=False)
            return pe.matmul(dst, lo, x_hi, start=False, stop=stop)

        def down(c, p):
            g = PAIRS * c + p
            if p == 0:
                after(pe, y_made, c)
            after(pe, hi_made, g + 1)
            after(pe, lo_made, g + 1)
            b = p % HSPLIT
            three(y_bank, w["d_hi"][:, p, :], w["d_lo"][:, p, :], hid_hi[:, b, :], hid_lo[:, b, :],
                  p == 0, p == PAIRS - 1).then_inc(down_done, 1)

        def step(name, c, par):
            nxt = 1 - par
            after(pe, misc_read, count("turn_n", c) if name in ("k", "v") else count(name, c) - 1)
            if name == "add":
                after(pe, y_made, c)
                for i in range(TILES):
                    last = pe.transpose(misc[:, i * P:i * P + P], y_sb[:, i * P:i * P + P], ident[:])
            elif name in ("turn_x", "turn_n"):
                ln, k = (ln_f, c + 2) if name == "turn_x" else (ln_q, c)
                after(pe, ln["xn_made"], 2 * k)
                for i in range(TILES):
                    last = pe.transpose(misc[:, i * P:i * P + P], ln["xn"][:, i, :], ident[:])
            elif name == "route":
                for i in range(TILES):
                    s = slice(i * P, i * P + P)
                    o = misc[:, i * EXPERTS:(i + 1) * EXPERTS]
                    pe.matmul(o, x_t[:, nxt, 0, s], w["r_hi"][:], start=True, stop=False)
                    pe.matmul(o, x_t[:, nxt, 1, s], w["r_hi"][:], start=False, stop=False)
                    last = pe.matmul(o, x_t[:, nxt, 0, s], w["r_lo"][:], start=False, stop=True)
            elif name in "qkv":
                m = "qkv".index(name)
                last = pe.matmul(bank[:, PROJ_BANK[name], :], w["qkv_t"][:, m * P:m * P + P], x2_t[:],
                                 start=True, stop=True)
            elif name == "turn_w":
                after(pe, wn_made, c + 2)
                for i in range(TILES):
                    last = pe.transpose(misc[0:EXPERTS, i * P:i * P + P], wn[:, i, :], ident[:])
            elif name == "turn_v":
                for i in range(TILES):
                    last = pe.transpose(misc[:, i * P:i * P + P], v_t[:, i * P:i * P + P], ident[:])
            last.then_inc(misc_ready, 1)

        def slot(c, par, p):
            g = PAIRS * c + p
            b = p % 2
            x_hi, x_lo = x_t[:, par, 0, :], x_t[:, par, 1, :]
            if p == 0:
                after(pe, misc_read, before(c))
            after(pe, scaled_made, g - 1)
            three(bank[:, UP_BANK + b, :], w["u_hi"][:, p, :], w["u_lo"][:, p, :],
                  x_hi, x_lo, True, True).then_inc(up_ready, 1)
            after(pe, hid_made, g - 1)
            three(bank[:, GATE_BANK + b, :], w["g_hi"][:, p, :], w["g_lo"][:, p, :],
                  x_hi, x_lo, True, True).then_inc(gate_ready, 1)
            if p >= LAG:
                down(c, p - LAG)
            elif not is_first(c):
                down(c - 1, PAIRS - LAG + p)
            for name in setup_at(c, p):
                setup.tensor(pe, name)
            for name in steps_at(c, p, 0):
                step(name, c, par)

        def ahead(*names):
            for name in names:
                if name in SETUP:
                    setup.tensor(pe, name)
                else:
                    step(name, -1, 1)

        def main():
            on_chunks(pe, slot)
            for p in range(PAIRS - LAG, PAIRS):
                down(CHUNKS - 1, p)
            for name in last_steps:
                step(name, CHUNKS, CHUNKS % 2)

        return Parts(ahead, main)

    def scalar(act):
        def copy_y(c):
            after(act, down_done, PAIRS * c)
            if isinstance(c, int) and c == CHUNKS:
                act.wait_ge(misc_ready, count("add", c - 1))
            act.activation(y_sb[:], y_bank, ACT.Copy).then_inc(y_made, 1)

        def read(name, c, par):
            n = count(name, c)
            nxt = 1 - par
            if name == "turn_x":
                after(act, misc_ready, n)
                act.activation(x_t[:, nxt, 0, :], misc, ACT.Copy).then_inc(misc_half, 1)
            elif name == "turn_w":
                after(act, misc_ready, n)
                after(act, comb_stored, 16 * (c + 1))
                act.activation(comb_t[:], misc[0:EXPERTS, :], ACT.Copy).then_inc(misc_read, 1)
            elif name == "turn_n":
                after(act, misc_ready, n)
                act.activation(x2_t[:], misc, ACT.Copy).then_inc(misc_read, 1)
            elif name in ("q", "k"):
                hold(act, proj_stats_made, 3 * (c - 1) + "qkv".index(name) + 1)
                act.activation(rows(qkv[name], c - 1).rearrange("p a b -> p (a b)"), bank[:, PROJ_BANK[name], :],
                               ACT.Copy).then_inc(misc_read, 1)
            elif name == "v":
                after(act, proj_stats_made, 3 * (c - 1) + 3)
                act.activation(v_t[:], bank[:, PROJ_BANK[name], :], ACT.Copy).then_inc(misc_read, 1)
            elif name == "turn_v":
                hold(act, misc_ready, n)
                act.activation(rows(qkv["v"], c - 1).rearrange("p a b -> p (a b)"), misc,
                               ACT.Copy).then_inc(misc_read, 1)

        def split_hi(g, p):
            after(act, hid_made, g + 1)
            after(act, down_done, g + 1 - HSPLIT)
            act.activation(hid_hi[:, p % HSPLIT, :], hid[:, p % 2, :], ACT.Copy).then_inc(hi_made, 1)

        def ln_apply(ln, chunk, k, part):
            hold(act, ln["shift_made"], k + 1)
            x = rows(x_sb, chunk)
            for i in range(part * TILES // 2, (part + 1) * TILES // 2):
                last = act.activation(ln["xn"][:, i, :], x[:, i, :], ACT.Identity, scale=ln["rstd"][:, i, :],
                                      bias=ln["shift"][:, i, :])
            last.then_inc(ln["xn_made"], 1)

        def tanh_z(k):
            after(act, z_made, k + 1)
            act.activation(th[:], z[:], ACT.Tanh, scale=0.5).then_inc(th_made, 1)

        def exp_z():
            act.wait_ge(z_made, 1)
            act.activation(th[:], z[:], ACT.Exp).then_inc(th_made, 1)

        def slot(c, par, p):
            g = PAIRS * c + p
            for name in setup_at(c, p - 1):
                setup.scalar(act, name)
            for name in steps_at(c, p, 1):
                read(name, c, par)
            follows = not isinstance(c, int) or c < CHUNKS - 1
            if follows and p in (2, 4):
                ln_apply(ln_f, c + 1, c + 1, p // 2 - 1)
            if follows and p == 7:
                tanh_z(c + 1)
            if qkv and not is_first(c) and p in (11, 12):
                ln_apply(ln_q, c - 1, c - 1, p - 11)
            after(act, gate_ready, g + 1)
            gate_bank = bank[:, GATE_BANK + p % 2, :]
            act.activation(gate_bank, gate_bank, ACT.Silu).then_inc(silu_made, 1)
            if p == LAG - 1 and not is_first(c):
                copy_y(c)
            if not (is_first(c) and p == 0):
                split_hi(g - 1, (p - 1) % PAIRS)

        def ahead(*names):
            for name in names:
                if name == "tanh":
                    tanh_z(0)
                elif name == "exp":
                    exp_z()
                elif name == "apply":
                    for part in range(2):
                        ln_apply(ln_f, 0, 0, part)
                elif name in SETUP:
                    setup.scalar(act, name)
                else:
                    read(name, -1, 1)

        def main():
            on_chunks(act, slot)
            split_hi(PAIRS * CHUNKS - 1, PAIRS - 1)
            copy_y(CHUNKS)
            if qkv:
                for part in range(2):
                    ln_apply(ln_q, CHUNKS - 1, CHUNKS - 1, part)
            for name in last_steps:
                read(name, CHUNKS, CHUNKS % 2)

        return Parts(ahead, main)

    def vector(dve):
        def ln_stats(ln, chunk, k, also=None, part=None):
            if also is not None:
                hold(dve, misc_read, also)
            elif setup and isinstance(chunk, int) and chunk < 2:
                dve.wait_ge(setup.x_in[chunk], 16)
            x = rows(x_sb, chunk)
            tiles = range(TILES) if part is None else range(part * TILES // 2, (part + 1) * TILES // 2)
            for i in tiles:
                last = dve.bn_stats(ln["stats"][:, i, :], x[:, i, :])
            if part == 0:
                return
            last.then_inc(ln["stats_made"], 1)
            hold(dve, ln["stats_made"], k + 1)
            for i in range(TILES):
                last = dve.bn_aggr(ln["mv"][:, i, :], ln["stats"][:, i, :])
            last.then_inc(ln["mv_made"], 1)

        def ln_shift(ln, k):
            after(dve, ln["rstd_made"], k + 1)
            dve.scalar_tensor_tensor(out=ln["shift"][:], in0=ln["mv"][:, :, 0:1], scalar=-1.0, in1=ln["rstd"][:],
                                     op0=ALU.mult, op1=ALU.mult).then_inc(ln["shift_made"], 1)

        def pick(c, part):
            k = c + 1
            if part == 1:
                for i in range(TILES):
                    last = dve.match_replace(rest[:, i, :], top[:, i, :], logits[:, i, :], MASKED)
                last.then_inc(rest_made, 1)
                after(dve, rest_made, k + 1)
                dve.tensor_tensor(chosen[:], logits[:], rest[:], ALU.not_equal).then_inc(chosen_made, 1)
                return
            after(dve, misc_ready, count("route", c))
            dve.tensor_copy(logits[:].rearrange("p a b -> p (a b)"),
                            misc[:, 0:TILES * EXPERTS]).then_inc(misc_read, 1)
            hold(dve, misc_read, count("route", c))
            for i in range(TILES):
                last = dve.max(top[:, i, :], logits[:, i, :])
            last.then_inc(top_made, 1)
            after(dve, top_made, k + 1)
            dve.tensor_tensor(z[:], logits[:], top[:, :, 0:1].to_broadcast([P, TILES, EXPERTS]),
                              ALU.subtract).then_inc(z_made, 1)

        def weigh(c, part, exp=False):
            k = c + 1
            if part == 0 and exp:
                dve.memset(den[:], 1.0).then_inc(den_made, 1)
                dve.memset(den_inv[:], 1.0).then_inc(den_inv_made, 1)
                after(dve, th_made, k + 1)
                after(dve, chosen_made, k + 1)
                dve.tensor_tensor(num[:], th[:], chosen[:], ALU.mult).then_inc(num_made, 1)
            elif part == 0:
                after(dve, th_made, k + 1)
                dve.tensor_scalar(den[:], th[:], -1.0, 1.0, ALU.mult, ALU.add).then_inc(den_made, 1)
                after(dve, chosen_made, k + 1)
                dve.scalar_tensor_tensor(out=num[:], in0=th[:], scalar=1.0, in1=chosen[:],
                                         op0=ALU.add, op1=ALU.mult).then_inc(num_made, 1)
            elif part == 1 and not exp:
                after(dve, den_made, k + 1)
                dve.reciprocal(den_inv[:], den[:]).then_inc(den_inv_made, 1)
            elif part == 2:
                after(dve, num_made, k + 1)
                after(dve, den_inv_made, k + 1)
                dve.tensor_tensor(wt[:], num[:], den_inv[:], ALU.mult).then_inc(wt_made, 1)
                after(dve, wt_made, k + 1)
                dve.tensor_reduce(wsum[:], wt[:], AX_X, ALU.add).then_inc(wsum_made, 1)
                after(dve, wsum_made, k + 1)
                dve.reciprocal(winv[:], wsum[:]).then_inc(winv_made, 1)
                after(dve, winv_made, k + 1)
                dve.scalar_tensor_tensor(out=wn[:], in0=wt[:], scalar=0.5,
                                         in1=winv[:].to_broadcast([P, TILES, EXPERTS]),
                                         op0=ALU.mult, op1=ALU.mult).then_inc(wn_made, 1)

        def read(name, c, par):
            n = count(name, c)
            nxt = 1 - par
            if name == "add":
                x = rows(x_sb, c - 1)
                after(dve, misc_ready, n)
                dve.tensor_tensor(x, misc.rearrange("p (a b) -> p a b", a=TILES), x,
                                  ALU.add).then_inc(misc_read, 1)
            elif name == "turn_x":
                after(dve, misc_half, c + 2)
                dve.tensor_tensor(x_t[:, nxt, 1, :], misc, x_t[:, nxt, 0, :].bitcast(F32),
                                  ALU.subtract).then_inc(misc_read, 1)
            elif name == "route":
                pick(c, 0)
            elif name in ("q", "k", "v"):
                m = "qkv".index(name)
                hold(dve, misc_ready, n)
                at = c - 1 + CHUNKS * m
                dst = w["proj_stats"][:, at, :] if isinstance(at, int) else w["proj_stats"][:, bass.ds(at, 1), :]
                dve.bn_stats(dst, bank[:, PROJ_BANK[name], :]).then_inc(proj_stats_made, 1)

        def slot(c, par, p):
            g = PAIRS * c + p
            b = p % 2
            for name in setup_at(c, p - 1):
                setup.vector(dve, name)
            for name in steps_at(c, p, 1):
                read(name, c, par)
            follows = not isinstance(c, int) or c < CHUNKS - 1
            if follows and p == 0:
                ln_stats(ln_f, c + 1, c + 1)
            if setup and is_first(c) and p == PAIRS - 1:
                dve.wait_ge(setup.x_in[2], 16)
            if follows and p == 2:
                ln_shift(ln_f, c + 1)
            if follows and p == 7:
                pick(c, 1)
            if follows and p in (8, 9, 10):
                weigh(c, p - 8)
            if qkv and not is_first(c):
                if p in (7, 8):
                    ln_stats(ln_q, c - 1, c - 1, count("add", c), p - 7)
                if p == 10:
                    ln_shift(ln_q, c - 1)
            if p % GROUP == 0:
                q = p // GROUP
                after(dve, share_in[q % 2], 32 * (2 * c + q // 2 + 1))
            after(dve, up_ready, g + 1)
            after(dve, hid_made, g - 1)
            dve.tensor_tensor(scaled[:, b, :], bank[:, UP_BANK + b, :],
                              share[:, p // GROUP % 2, p % GROUP, :], ALU.mult).then_inc(scaled_made, 1)
            after(dve, scaled_made, g + 1)
            after(dve, silu_made, g + 1)
            after(dve, lo_made, g - 1)
            dve.tensor_tensor(hid[:, b, :], bank[:, GATE_BANK + b, :], scaled[:, b, :],
                              ALU.mult).then_inc(hid_made, 1)

        def ahead(*names):
            for name in names:
                if name == "stats":
                    if final is not None:
                        dve.wait_ge(final, 1)
                    ln_stats(ln_f, 0, 0)
                elif name == "shift":
                    ln_shift(ln_f, 0)
                elif name in ("weigh", "weigh_exp"):
                    for part in range(3):
                        weigh(-1, part, name == "weigh_exp")
                elif name == "route":
                    pick(-1, 0)
                    pick(-1, 1)
                elif name in SETUP:
                    setup.vector(dve, name)
                else:
                    read(name, -1, 1)

        def main():
            on_chunks(dve, slot)
            read("add", CHUNKS, 0)
            if qkv:
                ln_stats(ln_q, CHUNKS - 1, CHUNKS - 1, count("add", CHUNKS))
                ln_shift(ln_q, CHUNKS - 1)
                for name in ("q", "k", "v"):
                    read(name, CHUNKS, 0)

        return Parts(ahead, main)

    def gpsimd(pool):
        def rstd(ln, k):
            after(pool, ln["mv_made"], k + 1)
            pool.tensor_tensor(ln["ve"][:], ln["mv"][:, :, 1:2], w["eps"][:], ALU.add).then_inc(ln["ve_made"], 1)
            after(pool, ln["ve_made"], k + 1)
            pool.tensor_tensor(ln["rstd"][:], ln["ve"][:], w["neg_half"][:], ALU.pow).then_inc(ln["rstd_made"], 1)

        def slot(c, par, p):
            g = PAIRS * c + p
            follows = not isinstance(c, int) or c < CHUNKS - 1
            if follows and p == 0:
                rstd(ln_f, c + 1)
            if qkv and not is_first(c) and p == 8:
                rstd(ln_q, c - 1)
            after(pool, hi_made, g + 1)
            pool.tensor_tensor(hid_lo[:, p % HSPLIT, :], hid[:, p % 2, :],
                               hid_hi[:, p % HSPLIT, :].bitcast(F32), ALU.subtract).then_inc(lo_made, 1)

        def ahead():
            rstd(ln_f, 0)

        def main():
            on_chunks(pool, slot)
            if qkv:
                rstd(ln_q, CHUNKS - 1)

        return Parts(ahead, main)

    def sync(sp):
        def send_comb(k, par):
            hold(sp, misc_read, count("turn_w", k - 1))
            sp.dma_start(comb_d[par], comb_t[:]).then_inc(comb_stored, 16)

        def spread(c, par, q):
            if q == 0:
                hold(sp, comb_stored, 16 * (c + 1))
            hold(sp, scaled_made, PAIRS * c + GROUP * (q - 1))
            for half in range(2):
                src = comb_d[par].rearrange("(n two) t -> two n t", two=2)[half, GROUP * q:GROUP * q + GROUP, :]
                sp.dma_start(share[half * EDIM:half * EDIM + EDIM, q % 2, :, :],
                             src.partition_broadcast(EDIM)).then_inc(share_in[q % 2], 16)

        def store(c):
            hold(sp, misc_read, count("add", c))
            dst = out[c - 1] if isinstance(c, int) else out[bass.ds(c - 1, 1)].rearrange("a t h -> (a t) h")
            sp.dma_start(dst.rearrange("(n p) h -> p n h", p=P), rows(x_sb, c - 1)).then_inc(stored, 16)

        def chunk(c, par):
            spread(c, par, 2)
            if out is not None and not is_first(c):
                store(c)
            spread(c, par, 3)
            if not isinstance(c, int) or c < CHUNKS - 1:
                send_comb(c + 1, 1 - par)
                spread(c + 1, 1 - par, 0)
                spread(c + 1, 1 - par, 1)

        def main():
            send_comb(0, 0)
            spread(0, 0, 0)
            spread(0, 0, 1)
            chunk(0, 0)
            with sp.Fori(0, (CHUNKS - 2) // UNROLL) as k:
                for u in range(1, 1 + UNROLL):
                    chunk(k * UNROLL + u, u % 2)
            chunk(CHUNKS - 1, (CHUNKS - 1) % 2)
            if out is not None:
                store(CHUNKS)
                sp.wait_ge(stored, 16 * CHUNKS)

        return Parts(None, main)

    phase = Phase(tensor, scalar, vector, gpsimd, sync)
    phase.misc_read, phase.steps, phase.proj_stats_made = misc_read, before(CHUNKS) + N_PREV, proj_stats_made
    return phase


def attention_phase(ctx, nc, w, x_sb, bank, buf, qkv, before_it):
    def sb(name, shape, dt=F32):
        return ctx.enter_context(nc.sbuf_tensor(name, shape, dt))

    def sem(name):
        return ctx.enter_context(nc.semaphore(name))

    bn_mv = sb("bn_mv", [P, 3, 2])
    bn_ve = sb("bn_ve", [P, 3, 1])
    bn_rstd = sb("bn_rstd", [P, 3, 1])
    bn_scale = sb("bn_scale", [P, 3])
    bn_mean = sb("bn_mean", [P, 3])
    bn_shift = sb("bn_shift", [P, 3])
    q_scale = sb("q_scale", [P, 1])
    q_shift = sb("q_shift", [P, 1])
    v_shift = sb("v_shift", [P, P])
    out_v = sb("out_v", [P, P])
    shift_row = sb("shift_row", [P, P])
    q_n, k_n, y_sb = qkv["x2_t"], qkv["v_t"], buf["y_sb"]
    v_n = sb("v_n", [P, TILES, P])
    probs = sb("probs", [P, TILES, CHUNK])
    probs_t = sb("probs_t", [P, TILES, CHUNK])
    low = sb("low", [P, TILES])
    psum_row = sb("psum_row", [P, TILES])
    inv_row = sb("inv_row", [P, TILES])

    bn_step = sem("bn_step")
    bn_ve_made = sem("bn_ve_made")
    bn_rstd_made = sem("bn_rstd_made")
    shift_ready = sem("shift_ready")
    shift_made = sem("shift_made")
    shift_added = sem("shift_added")
    q_made = sem("q_made")
    k_made = sem("k_made")
    v_made = sem("v_made")
    s_ready = sem("s_ready")
    low_made = sem("low_made")
    exp_made = sem("exp_made")
    t_ready = sem("t_ready")
    even_made = sem("even_made")
    odd_made = sem("odd_made")
    y_ready = sem("y_ready")
    y_made = sem("y_made")
    o_ready = sem("o_ready")
    inv_made = sem("inv_made")
    x_done = sem("x_done")
    T_BANK, Y_BANK = 4, 6
    y_bank = o_bank = bank[:, Y_BANK, :]
    SCALE = float(P) ** -0.5

    def on_rows(eng, part, ahead):
        for b in (-1, 0):
            part(b)
        with eng.Fori(1, CHUNKS // 2) as b:
            part(b)
        ahead("part 3 done")
        for b in range(CHUNKS // 2, CHUNKS):
            part(b)
            ahead(f"part {b} done")
        part(CHUNKS)

    def midst(b, ahead):
        if isinstance(b, int) and CHUNKS // 2 <= b < CHUNKS:
            ahead(f"in part {b}")

    def runs(b):
        return not isinstance(b, int) or 0 <= b < CHUNKS

    def scored(b):
        return not isinstance(b, int) or b + 1 < CHUNKS

    def has_last(b):
        return not isinstance(b, int) or b >= 1

    def flat(t, b):
        return rows(t, b).rearrange("p a b -> p (a b)")

    def tensor(pe, ahead):
        pe.wait_ge(before_it.misc_read, before_it.steps)
        pe.wait_ge(bn_step, 9)
        pe.matmul(o_bank[:, 0:P], v_shift[:], w["out_t"][:], start=True, stop=True).then_inc(shift_ready, 1)

        def turn(b, j):
            if j == 0:
                after(pe, exp_made, TILES * b + TILES)
            after(pe, (even_made, odd_made)[j % 2], 2 * b + j // 2)
            for i in range(j, TILES):
                last = pe.transpose(bank[:, T_BANK + j % 2, i * P:i * P + P], probs[:, i, j * P:j * P + P],
                                    w["ident"][:])
            last.then_inc(t_ready, 1)

        def scores(b, i):
            if i == 0:
                after(pe, q_made, b + 1)
                after(pe, k_made, b + 1)
            after(pe, exp_made, TILES * (b - 1) + i + 1)
            n = i * P + P
            if i:
                pe.matmul(bank[:, i, 0:i * P], q_n[:, i * P:n], k_n[:, 0:i * P], start=True, stop=True)
            pe.matmul(bank[:, i, i * P:n], q_n[:, i * P:n], k_n[:, i * P:n], start=True, stop=False)
            pe.matmul(bank[:, i, i * P:n], w["ident_b"][:], w["causal_b"][:], start=False,
                      stop=True).then_inc(s_ready, 1)

        def part(b):
            if runs(b):
                turn(b, 0)
                turn(b, 1)
            if has_last(b):
                after(pe, y_made, b)
                for i in range(TILES):
                    last = pe.matmul(o_bank[:, i * P:i * P + P], y_sb[:, i * P:i * P + P], out_v[:],
                                     start=True, stop=True)
                last.then_inc(o_ready, 1)
            if scored(b):
                scores(b + 1, 0)
                scores(b + 1, 1)
            if runs(b):
                turn(b, 2)
                turn(b, 3)
            if scored(b):
                scores(b + 1, 2)
                scores(b + 1, 3)
            midst(b, ahead)
            if runs(b):
                after(pe, v_made, b + 1)
                after(pe, x_done, b)
                for j in range(TILES):
                    after(pe, (even_made, odd_made)[j % 2], 2 * b + j // 2 + 1)
                    last = pe.matmul(y_bank[:, j * P:CHUNK], v_n[:, j, :], probs_t[:, j, j * P:CHUNK],
                                     start=(j == 0), stop=True, skip_group_check=(j > 0))
                last.then_inc(y_ready, 1)

        pe.wait_ge(shift_made, 1)
        on_rows(pe, part, ahead)

    def scalar(act, ahead):
        act.wait_ge(shift_ready, 1)
        act.activation(shift_row[:], o_bank[:, 0:P], ACT.Copy).then_inc(shift_made, 1)
        act.wait_ge(bn_step, 9)

        def exps(b, i):
            after(act, low_made, TILES * b + i + 1)
            after(act, t_ready, TILES * (b - 1) + i + 1)
            after(act, inv_made, b)
            n = i * P + P
            act.activation(probs[:, i, 0:n], bank[:, i, 0:n], ACT.Exp, scale=-1.0, bias=low[:, i:i + 1],
                           accum_out=psum_row[:, i:i + 1]).then_inc(exp_made, 1)

        def odd(b, j):
            after(act, t_ready, TILES * b + j + 1)
            after(act, y_ready, b)
            act.activation(probs_t[:, j, j * P:CHUNK], bank[:, T_BANK + 1, j * P:CHUNK],
                           ACT.Copy).then_inc(odd_made, 1)

        def part(b):
            if scored(b):
                hold(act, s_ready, TILES * (b + 1))
                act.activation(q_n[:], flat(qkv["q"], b + 1), ACT.Identity, scale=q_scale[:],
                               bias=q_shift[:]).then_inc(q_made, 1)
            if runs(b):
                odd(b, 1)
            if scored(b):
                exps(b + 1, 0)
                exps(b + 1, 1)
            midst(b, ahead)
            if runs(b):
                odd(b, 3)
            if scored(b):
                exps(b + 1, 2)
                exps(b + 1, 3)
            if runs(b):
                after(act, y_ready, b + 1)
                after(act, o_ready, b)
                act.activation(y_sb[:], y_bank, ACT.Copy).then_inc(y_made, 1)

        on_rows(act, part, ahead)

    def vector(dve, ahead):
        dve.wait_ge(before_it.proj_stats_made, 3 * CHUNKS)
        for m in range(3):
            last = dve.bn_aggr(bn_mv[:, m, :], w["proj_stats"][:, m * CHUNKS:(m + 1) * CHUNKS, :])
        last.then_inc(bn_step, 1)
        dve.wait_ge(bn_rstd_made, 1)
        col = lambda t: t[:].rearrange("p (a b) -> p a b", b=1)
        dve.tensor_tensor(col(bn_scale), w["gamma_beta"][:, 0:3].rearrange("p (a b) -> p a b", b=1), bn_rstd[:], ALU.mult).then_inc(bn_step, 1)
        dve.wait_ge(bn_step, 2)
        dve.tensor_tensor(col(bn_mean), bn_mv[:, :, 0:1], col(bn_scale), ALU.mult).then_inc(bn_step, 1)
        dve.wait_ge(bn_step, 3)
        dve.tensor_tensor(bn_shift[:], w["gamma_beta"][:, 3:6], bn_mean[:], ALU.subtract).then_inc(bn_step, 1)
        dve.wait_ge(bn_step, 4)
        dve.tensor_scalar(q_scale[:], bn_scale[:, 0:1], -SCALE, None, ALU.mult).then_inc(bn_step, 1)
        dve.tensor_scalar(q_shift[:], bn_shift[:, 0:1], -SCALE, None, ALU.mult).then_inc(bn_step, 1)
        dve.tensor_scalar(out_v[:], w["out_t"][:], bn_scale[:, 2:3], None, ALU.mult).then_inc(bn_step, 1)
        dve.tensor_copy(v_shift[:], bn_shift[:, 2:3].to_broadcast([P, P])).then_inc(bn_step, 1)
        dve.memset(low[:], 0.0).then_inc(bn_step, 1)
        dve.wait_ge(bn_step, 9)

        def even(b, j):
            after(dve, t_ready, TILES * b + j + 1)
            after(dve, y_ready, b)
            dve.tensor_copy(probs_t[:, j, j * P:CHUNK], bank[:, T_BANK, j * P:CHUNK]).then_inc(even_made, 1)

        def lows(b, i):
            after(dve, s_ready, TILES * b + i + 1)
            after(dve, exp_made, TILES * (b - 1) + i + 1)
            dve.tensor_reduce(low[:, i:i + 1], bank[:, i, 0:i * P + P], AX_X, ALU.min).then_inc(low_made, 1)

        def part(b):
            if scored(b):
                after(dve, s_ready, TILES * (b + 1))
                dve.tensor_scalar(k_n[:], flat(qkv["k"], b + 1), bn_scale[:, 1:2], bn_shift[:, 1:2],
                                  ALU.mult, ALU.add).then_inc(k_made, 1)
            if runs(b):
                even(b, 0)
            if has_last(b):
                dve.wait_ge(shift_added, 1)
                hold(dve, o_ready, b)
                hold(dve, inv_made, b)
                x = rows(x_sb, b - 1)
                for i in range(TILES):
                    last = dve.scalar_tensor_tensor(out=x[:, i, :], in0=o_bank[:, i * P:i * P + P],
                                                    scalar=inv_row[:, i:i + 1], in1=x[:, i, :],
                                                    op0=ALU.mult, op1=ALU.add)
                last.then_inc(x_done, 1)
            if runs(b):
                after(dve, exp_made, TILES * b + TILES)
                after(dve, x_done, b)
                dve.reciprocal(inv_row[:], psum_row[:]).then_inc(inv_made, 1)
            if scored(b):
                lows(b + 1, 0)
                lows(b + 1, 1)
            midst(b, ahead)
            if runs(b):
                even(b, 2)
            if scored(b):
                lows(b + 1, 2)
                lows(b + 1, 3)

        dve.wait_ge(before_it.misc_read, before_it.steps)
        on_rows(dve, part, ahead)

    def gpsimd(pool, ahead):
        pool.wait_ge(bn_step, 1)
        pool.tensor_tensor(bn_ve[:], bn_mv[:, :, 1:2], w["eps"][:, 0:3, :], ALU.add).then_inc(bn_ve_made, 1)
        pool.wait_ge(bn_ve_made, 1)
        pool.tensor_tensor(bn_rstd[:], bn_ve[:], w["neg_half"][:, 0:3, :], ALU.pow).then_inc(bn_rstd_made, 1)

        def copy_v(b):
            hold(pool, y_ready, b)
            pool.tensor_copy(v_n[:], rows(qkv["v"], b)).then_inc(v_made, 1)

        pool.wait_ge(before_it.misc_read, before_it.steps)
        copy_v(0)
        pool.wait_ge(shift_made, 1)
        pool.tensor_tensor(x_sb[:], x_sb[:], shift_row[:].rearrange("p (a b) -> p a b", a=1)
                           .to_broadcast([P, TILES * CHUNKS, P]), ALU.add).then_inc(shift_added, 1)
        with pool.Fori(1, CHUNKS // 2 + 1) as b:
            copy_v(b)
        ahead()
        with pool.Fori(CHUNKS // 2 + 1, CHUNKS) as b:
            copy_v(b)

    phase = Phase(tensor, scalar, vector, gpsimd, None)
    phase.x_done = x_done
    return phase


def build(nc, x, W_attn, W_proj, lora_attn_A, lora_attn_B, lora_proj_A, lora_proj_B, gamma, beta, gate, gate_up,
          down, out):
    d = {"x": x, "W_attn": W_attn, "W_proj": W_proj, "lora_attn_A": lora_attn_A, "lora_attn_B": lora_attn_B,
         "lora_proj_A": lora_proj_A, "lora_proj_B": lora_proj_B, "gamma": gamma, "beta": beta, "gate": gate,
         "gate_up": gate_up, "down": down}
    with ExitStack() as ctx:
        def sb(name, shape, dt=F32):
            return ctx.enter_context(nc.sbuf_tensor(name, shape, dt))

        bank = ctx.enter_context(nc.psum_tensor("bank", [P, 8, CHUNK], F32))
        x_sb = sb("x_sb", [P, CHUNKS * TILES, P])
        w = {n: sb(n, [P, PAIRS, P], F32R) for n in ("g_hi", "g_lo", "u_hi", "u_lo", "d_hi", "d_lo")}
        w |= {n: sb(n, [P, EXPERTS], F32R) for n in ("r_hi", "r_lo")}
        w |= {"qkv_t": sb("qkv_t", [P, 3 * P]), "nothing": sb("nothing", [P, 1]), "out_t": sb("out_t", [P, P]), "ident": sb("ident", [P, P]),
              "ident_b": sb("ident_b", [P, P], mybir.dt.bfloat16),
              "causal_b": sb("causal_b", [P, P], mybir.dt.bfloat16),
              "gamma_beta": sb("gamma_beta", [P, 6]),
              "eps": sb("eps", [P, TILES, 1]), "neg_half": sb("neg_half", [P, TILES, 1]),
              "proj_stats": sb("proj_stats", [P, 3 * CHUNKS, 6])}
        qkv = {n: sb(f"{n}_all", [P, CHUNKS * TILES, P]) for n in "qkv"}
        qkv |= {"x2_t": sb("x2_t", [P, CHUNK]), "v_t": sb("v_t", [P, CHUNK])}
        buf = ffn_buffers(ctx, nc)
        setup = setup_phase(ctx, nc, d, w, x_sb, bank, qkv)
        ffn_a = ffn_phase(ctx, nc, "a", w, x_sb, bank, buf, qkv=qkv, setup=setup)
        attn = attention_phase(ctx, nc, w, x_sb, bank, buf, qkv, ffn_a)
        ffn_c = ffn_phase(ctx, nc, "c", w, x_sb, bank, buf, final=attn.x_done, out=out)
        block = ctx.enter_context(nc.Block())

        def between(parts, steps):
            return lambda place: parts.ahead(*steps.get(place, ()))

        @block.sync
        def _(sp):
            setup.sync(sp)
            ffn_a.sync(sp).main()
            ffn_c.sync(sp).main()

        @block.gpsimd
        def _(pool):
            setup.gpsimd(pool)
            a, c = ffn_a.gpsimd(pool), ffn_c.gpsimd(pool)
            a.ahead()
            a.main()
            attn.gpsimd(pool, c.ahead)
            c.main()

        @block.scalar
        def _(act):
            a, c = ffn_a.scalar(act), ffn_c.scalar(act)
            setup.loads(act)
            a.ahead("apply", "gate", "turn_x", "gu0", "tanh", "turn_w")
            a.main()
            attn.scalar(act, between(c, {"in part 4": ["apply"], "part 4 done": ["turn_x"],
                                         "part 5 done": ["exp"], "in part 7": ["turn_w"]}))
            c.main()

        @block.vector
        def _(dve):
            dve.wait_ge(setup.const_step, 4)
            a, c = ffn_a.vector(dve), ffn_c.vector(dve)
            a.ahead("stats", "shift", "gate", "turn_x", "gu0", "route", "weigh")
            a.main()
            attn.vector(dve, between(c, {"part 3 done": ["stats"], "in part 4": ["shift"], "part 4 done": ["turn_x"],
                                         "part 5 done": ["route"], "part 6 done": ["weigh_exp"]}))
            c.main()

        @block.tensor
        def _(pe):
            a, c = ffn_a.tensor(pe), ffn_c.tensor(pe)
            a.ahead("gate", "turn_x", "gu0", "route", "turn_w")
            a.main()
            attn.tensor(pe, between(c, {"part 4 done": ["turn_x"], "in part 5": ["route"], "in part 7": ["turn_w"]}))
            c.main()


_INS = ["L0_attn_x", "L0_attn_W_attn", "L0_attn_W_proj", "L0_attn_lora_attn_A", "L0_attn_lora_attn_B",
        "L0_attn_lora_proj_A", "L0_attn_lora_proj_B", "L0_attn_bn_gamma", "L0_attn_bn_beta",
        "L0_ffn_gate_w", "L0_ffn_gate_up_w", "L0_ffn_down_w"]


def kernel(**inputs):
    import concourse.bacc as bacc
    from concourse.bass_utils import run_bass_kernel_spmd

    nc = bacc.Bacc("TRN2", target_bir_lowering=False, num_devices=1)
    arrays, args = {}, []
    for name in _INS:
        a = np.ascontiguousarray(inputs[name])
        arrays[name] = a
        args.append(nc.dram_tensor(name, a.shape, mybir.dt.from_np(a.dtype), kind="ExternalInput").ap())
    shape = arrays["L0_attn_x"].shape
    args.append(nc.dram_tensor("y_out", shape, F32, kind="ExternalOutput").ap())
    build(nc, *args)
    r = run_bass_kernel_spmd(nc, [arrays], core_ids=[0])
    return r.results[0]["y_out"]
```

```python
from contextlib import ExitStack

import numpy as np

import concourse.bass as bass
from concourse import mybir

F32 = mybir.dt.float32
F32R = mybir.dt.float32r
ALU = mybir.AluOpType
ACT = mybir.ActivationFunctionType
AX_X = mybir.AxisListType.X

P = 128
TILES = 4
CHUNK = TILES * P
CHUNKS = 8
EXPERTS = 32
EDIM = 64
PAIRS = EXPERTS // 2
TOPK = 8
EPS = 1e-5
MASKED = -1e30
LAG = 3
GROUP = 4
HSPLIT = 4
UNROLL = 2


class Phase:
    def __init__(self, tensor, scalar, vector, gpsimd, sync):
        self.tensor, self.scalar, self.vector, self.gpsimd, self.sync = tensor, scalar, vector, gpsimd, sync


class Parts:
    def __init__(self, ahead, main):
        self.ahead, self.main = ahead, main


def after(eng, sem, value):
    if not isinstance(value, int) or value > 0:
        eng.wait_ge(sem, value)


def hold(eng, sem, value):
    if isinstance(value, int):
        after(eng, sem, value)
    else:
        eng.wait_ge(sem, value)
        eng.nop(nofuse=True)


def rows(x_sb, c):
    return x_sb[:, TILES * c:TILES * c + TILES, :] if isinstance(c, int) else x_sb[:, bass.ds(TILES * c, TILES), :]


def setup_phase(ctx, nc, d, w, x_sb, bank, qkv):
    def sem(name):
        return ctx.enter_context(nc.semaphore(name))

    gu_nat = qkv["q"][:]
    flat_k = qkv["k"][:].rearrange("p a b -> p (a b)")
    dn_nat = flat_k[:, 0:EXPERTS * EDIM]
    attn_nat = qkv["k"][:, 16:19, :]
    proj_nat = qkv["k"][:, 19, :]
    gate_nat = qkv["k"][0:EXPERTS, 20, :]
    la_a = qkv["k"][:, 21, 0:EDIM]
    lp_a = qkv["k"][:, 21, EDIM:2 * EDIM]
    la_b = flat_k[0:EDIM, 22 * P:25 * P]
    lp_b = qkv["k"][0:EDIM, 25, :]
    bn_nat = qkv["k"][0:6, 26, :]
    la_at = qkv["k"][0:EDIM, 27, :]
    lp_at = qkv["k"][0:EDIM, 28, :]
    projm_t = qkv["k"][:, 29, :]
    delta = qkv["v"][:, 0:3, :].rearrange("p a b -> p (a b)")
    causal = qkv["v"][:, 3, :]
    qkv_f = qkv["v"][:, 8:11, :].rearrange("p a b -> p (a b)")
    sel = qkv["v"][:, 12:12 + GROUP * TILES, :]

    GUS = 8
    DNS = 4
    gu_in = [sem(f"gu_in{i}") for i in range(GUS)]
    dn_in = [sem(f"dn_in{i}") for i in range(DNS)]
    gate_in = sem("gate_in")
    small_in = sem("small_in")
    x_in = [sem(f"x_in{i}") for i in range(3)]
    const_step = sem("const_step")
    sel_step = sem("sel_step")
    turned = sem("turned")
    copied = sem("copied")
    passed = sem("passed")

    steps = {"gate": -1, "gu0": -1, "gu1": 0, "dn0": 1, "gu2": 2, "lora": 3, "gu3": 4, "dn1": 5, "gu4": 6,
             "attn": 7, "gu5": 8, "dn2": 9, "gu6": 10, "delta": 11, "gu7": 12, "dn3": 13, "projm": 14,
             "comb": 15}
    number = {name: n + 1 for n, name in enumerate(steps)}
    b = bank[:, 6, :]

    def sync(sp):
        def gu(q):
            src = d["gate_up"][4 * q:4 * q + 4].rearrange("e (i j) h -> (e i) j h", j=4)
            sp.dma_start(gu_nat[:, 4 * q:4 * q + 4, :], src).then_inc(gu_in[q], 16)

        def dn(q):
            n = EXPERTS // DNS
            sp.dma_start(dn_nat[:, q * n * EDIM:(q + 1) * n * EDIM].rearrange("h (e k) -> h e k", e=n),
                         d["down"][n * q:n * q + n].rearrange("e h k -> h e k")).then_inc(dn_in[q], 16)

        sp.dma_start(x_sb[:, 0:TILES, :], d["x"][0].rearrange("(n p) h -> p n h", p=P)).then_inc(x_in[0], 16)
        gu(0)
        gu(1)
        sp.dma_start(x_sb[:, TILES:2 * TILES, :], d["x"][1].rearrange("(n p) h -> p n h", p=P)).then_inc(x_in[1], 16)
        dn(0)
        gu(2)
        small_loads(sp)
        gu(3)
        dn(1)
        gu(4)
        gu(5)
        dn(2)
        gu(6)
        gu(7)
        dn(3)
        sp.dma_start(x_sb[:, 2 * TILES:, :].rearrange("p (c n) h -> p c n h", n=TILES),
                     d["x"][2:].rearrange("c (n p) h -> p c n h", p=P)).then_inc(x_in[2], 16)

    def loads(act):
        act.dma_start(gate_nat, d["gate"]).then_inc(gate_in, 16)

    def small_loads(sp):
        for dst, src in ((attn_nat, d["W_attn"].rearrange("(m p) c -> p m c", p=P)), (proj_nat, d["W_proj"]),
                         (la_a, d["lora_attn_A"]), (lp_a, d["lora_proj_A"]), (la_b, d["lora_attn_B"]),
                         (lp_b, d["lora_proj_B"]), (bn_nat[0:3, :], d["gamma"].rearrange("(m p) -> m p", p=P)),
                         (bn_nat[3:6, :], d["beta"].rearrange("(m p) -> m p", p=P))):
            sp.dma_start(dst, src).then_inc(small_in, 16)

    def halves(q):
        t = b.rearrange("h (j e f i) -> h f e i j", j=4, e=4, f=2)
        s = slice(2 * q, 2 * q + 2)
        for f, (hi, lo) in enumerate((("g_hi", "g_lo"), ("u_hi", "u_lo"))):
            yield t[:, f], *(w[n][:, s, :].rearrange("h a (b i j) -> h (a b) i j", b=2, j=4) for n in (hi, lo))

    def scalar(act, name):
        act.wait_ge(turned, number[name])
        if name[:2] == "gu":
            for t, hi, lo in halves(int(name[2])):
                i = act.activation(hi, t, ACT.Copy)
        elif name[:2] == "dn":
            q = int(name[2])
            i = act.activation(w["d_hi"][:, 4 * q:4 * q + 4, :].rearrange("p a b -> p (a b)"), b, ACT.Copy)
        elif name == "gate":
            i = act.activation(w["r"][:, 0, :], b[:, 0:EXPERTS], ACT.Copy)
        elif name == "lora":
            act.activation(la_at, b[0:EDIM, 0:P], ACT.Copy)
            i = act.activation(lp_at, b[0:EDIM, P:2 * P], ACT.Copy)
        elif name == "attn":
            act.activation(w["gamma_beta"][:], b[:, 3 * P:3 * P + 6], ACT.Copy)
            i = act.activation(qkv_f, b[:, 0:3 * P], ACT.Copy)
        elif name == "delta":
            i = act.activation(delta, b[:, 0:3 * P], ACT.Copy)
        elif name == "projm":
            act.activation(w["qkv"][:, 0, :], qkv_f, ACT.Copy)
            i = act.activation(projm_t, b[:, 0:P], ACT.Copy)
        elif name == "comb":
            i = act.activation(w["out_t"][:], b[:, 0:P], ACT.Copy)
        i.then_inc(copied, 1)

    def vector(dve, name):
        dve.wait_ge(copied, number[name])
        if name[:2] == "gu":
            for t, hi, lo in halves(int(name[2])):
                i = dve.tensor_tensor(lo, t, hi.bitcast(F32), ALU.subtract)
        elif name[:2] == "dn":
            q = int(name[2])
            s = slice(4 * q, 4 * q + 4)
            i = dve.tensor_tensor(w["d_lo"][:, s, :].rearrange("p a b -> p (a b)"), b,
                                  w["d_hi"][:, s, :].bitcast(F32).rearrange("p a b -> p (a b)"), ALU.subtract)
        elif name == "gate":
            i = dve.tensor_tensor(w["r"][:, 1, :], b[:, 0:EXPERTS], w["r"][:, 0, :].bitcast(F32), ALU.subtract)
        elif name == "delta":
            turned_rows = qkv_f.rearrange("c (r j) -> c r j", j=3)
            i = dve.tensor_tensor(turned_rows, delta.rearrange("c (j r) -> c r j", j=3), turned_rows, ALU.add)
        elif name == "projm":
            i = dve.tensor_tensor(w["qkv"][:, 1, :], qkv_f, w["qkv"][:, 0, :].bitcast(F32), ALU.subtract)
        else:
            i = dve.memset(w["nothing"][:], 0.0)
        i.then_inc(passed, 1)

    def gpsimd(pool):
        pool.memset(w["ident"][:], 0.0).then_inc(const_step, 1)
        pool.wait_ge(const_step, 1)
        pool.affine_select(out=w["ident"][:], in_=w["ident"][:], compare_op=ALU.not_equal, fill=1.0, base=0,
                           pattern=[[-1, P]], channel_multiplier=1).then_inc(const_step, 1)
        pool.memset(w["neg_half"][:], -0.5).then_inc(const_step, 1)
        pool.memset(w["eps"][:], EPS).then_inc(const_step, 1)
        pool.memset(causal, 0.0).then_inc(const_step, 1)
        pool.wait_ge(const_step, 5)
        pool.affine_select(out=causal, in_=causal, compare_op=ALU.is_ge, fill=-MASKED, base=0,
                           pattern=[[-1, P]], channel_multiplier=1).then_inc(const_step, 1)
        pool.wait_ge(const_step, 6)
        pool.tensor_copy(w["causal_b"][:], causal).then_inc(const_step, 1)
        pool.tensor_copy(w["ident_b"][:], w["ident"][:]).then_inc(const_step, 1)

    def selectors(pool):
        steps_p, steps_i = 2 * EDIM, EXPERTS * EDIM
        pool.memset(sel, 1.0).then_inc(sel_step, 1)
        pool.wait_ge(sel_step, 1)
        pool.affine_select(out=sel, in_=sel, compare_op=ALU.is_ge, fill=0.0, base=0,
                           pattern=[[steps_p, GROUP], [steps_i, TILES], [1, P]],
                           channel_multiplier=-EDIM).then_inc(sel_step, 1)
        pool.wait_ge(sel_step, 2)
        pool.affine_select(out=sel, in_=sel, compare_op=ALU.is_ge, fill=0.0, base=EDIM - 1,
                           pattern=[[-steps_p, GROUP], [-steps_i, TILES], [-1, P]],
                           channel_multiplier=EDIM).then_inc(sel_step, 1)

    def tensor(pe, name):
        ident = w["ident"]
        if name == "gate":
            pe.wait_ge(const_step, 2)
            pe.wait_ge(gate_in, 16)
        after(pe, passed, number[name] - 1)
        if name[:2] == "gu":
            q = int(name[2])
            pe.wait_ge(gu_in[q], 16)
            for j in range(4):
                i = pe.transpose(b[:, j * P:j * P + P], gu_nat[:, 4 * q + j, :], ident[:])
        elif name[:2] == "dn":
            q = int(name[2])
            pe.wait_ge(dn_in[q], 16)
            for e in range(4):
                n = 4 * q + e
                i = pe.transpose(b[:, e * P:e * P + P], dn_nat[:, n * P:n * P + P], ident[:])
        elif name == "gate":
            i = pe.transpose(b[:, 0:EXPERTS], gate_nat, ident[0:EXPERTS, 0:EXPERTS])
        elif name == "lora":
            pe.wait_ge(small_in, 16 * 8)
            pe.transpose(b[0:EDIM, 0:P], la_a, ident[:])
            i = pe.transpose(b[0:EDIM, P:2 * P], lp_a, ident[:])
        elif name == "attn":
            for m in range(3):
                pe.transpose(b[:, m * P:m * P + P], attn_nat[:, m, :], ident[:])
            i = pe.transpose(b[:, 3 * P:3 * P + 6], bn_nat, ident[0:6, 0:6])
        elif name == "delta":
            for j in range(3):
                i = pe.matmul(b[:, j * P:j * P + P], la_b[:, j * P:j * P + P], la_at, start=True, stop=True)
        elif name == "projm":
            pe.matmul(b[:, 0:P], proj_nat, ident[:], start=True, stop=False)
            i = pe.matmul(b[:, 0:P], lp_b, lp_at, start=False, stop=True)
        elif name == "comb":
            i = pe.matmul(b[:, 0:P], proj_nat, projm_t, start=True, stop=True)
        i.then_inc(turned, 1)

    setup = Phase(tensor, scalar, vector, gpsimd, sync)
    setup.steps, setup.loads, setup.x_in, setup.const_step = steps, loads, x_in, const_step
    setup.passed, setup.number = passed, number
    setup.sel, setup.sel_step, setup.selectors = sel, sel_step, selectors
    return setup


def ffn_buffers(ctx, nc):
    def sb(name, shape, dt=F32):
        return ctx.enter_context(nc.sbuf_tensor(name, shape, dt))

    def ln_set(name):
        return {"stats": sb(f"{name}_stats", [P, TILES, 6]), "mv": sb(f"{name}_mv", [P, TILES, 2]),
                "ve": sb(f"{name}_ve", [P, TILES, 1]), "rstd": sb(f"{name}_rstd", [P, TILES, 1]),
                "shift": sb(f"{name}_shift", [P, TILES, 1]),
                "xn": sb(f"{name}_xn", [P, TILES, P])}

    small = {n: sb(n, [P, TILES, EXPERTS]) for n in
             ("logits", "rest", "z", "chosen", "th", "den", "den_inv", "num", "wt", "wn")}
    return dict(
        ln_f=ln_set("lnf"), ln_q=ln_set("lnq"),
        x_t=sb("x_t", [P, 2, 2, CHUNK], F32R),
        comb_t=sb("comb_t", [P, P]),
        share=sb("share", [P, 2, GROUP, CHUNK]),
        scaled=sb("scaled", [P, 2, CHUNK]), hid=sb("hid", [P, 2, CHUNK]),
        hid_hi=sb("hid_hi", [P, HSPLIT, CHUNK], F32R), hid_lo=sb("hid_lo", [P, HSPLIT, CHUNK], F32R),
        y_sb=sb("y_sb", [P, CHUNK]), top=sb("top", [P, TILES, TOPK]),
        wsum=sb("wsum", [P, TILES, 1]), winv=sb("winv", [P, TILES, 1]), **small)


def ffn_phase(ctx, nc, tag, w, x_sb, bank, buf, qkv=None, setup=None, final=None, out=None):
    def sem(name):
        return ctx.enter_context(nc.semaphore(f"{name}_{tag}"))

    def ln_sems(name):
        return {n: sem(f"{name}_{n}") for n in ("stats_made", "mv_made", "ve_made", "rstd_made", "xn_made")}

    ln_f = buf["ln_f"] | ln_sems("lnf")
    ln_q = buf["ln_q"] | ln_sems("lnq") if qkv else None
    x_t, comb_t, share, scaled, hid = buf["x_t"], buf["comb_t"], buf["share"], buf["scaled"], buf["hid"]
    hid_hi, hid_lo, y_sb = buf["hid_hi"], buf["hid_lo"], buf["y_sb"]
    top, wsum, winv = buf["top"], buf["wsum"], buf["winv"]
    logits, rest, z, chosen, th = buf["logits"], buf["rest"], buf["z"], buf["chosen"], buf["th"]
    den, den_inv, num, wt, wn = buf["den"], buf["den_inv"], buf["num"], buf["wt"], buf["wn"]
    if qkv:
        x2_t = qkv["x2_t"]
    comb_d = nc.dram_tensor(f"comb_{tag}", [2, EXPERTS, CHUNK], F32, kind="Internal").ap()

    gate_ready = sem("gate_ready")
    up_ready = sem("up_ready")
    silu_made = sem("silu_made")
    scaled_made = sem("scaled_made")
    hid_made = sem("hid_made")
    comb_stored = sem("comb_stored")
    spread_ready = sem("spread_ready")
    share_in = [sem(f"share_in{i}") for i in range(2)]
    hi_made = sem("hi_made")
    lo_made = sem("lo_made")
    down_done = sem("down_done")
    y_made = sem("y_made")
    misc_ready = sem("misc_ready")
    misc_read = sem("misc_read")
    misc_half = sem("misc_half")
    shift_made = sem("shift_made_q")
    x2_hi_made = sem("x2_hi_made")
    top_made = sem("top_made")
    rest_made = sem("rest_made")
    z_made = sem("z_made")
    chosen_made = sem("chosen_made")
    th_made = sem("th_made")
    den_made = sem("den_made")
    den_inv_made = sem("den_inv_made")
    num_made = sem("num_made")
    wt_made = sem("wt_made")
    wsum_made = sem("wsum_made")
    winv_made = sem("winv_made")
    wn_made = sem("wn_made")
    proj_stats_made = sem("proj_stats_made")
    stored = sem("stored")

    GATE_BANK, UP_BANK, Y_BANK, MISC_BANK = 0, 2, 4, 7
    SPREAD_BANKS = (5, MISC_BANK)
    SHARE = 32
    y_bank = bank[:, Y_BANK, :]
    misc = bank[:, MISC_BANK, :]

    NEXT, PREV = 1, -1
    STEPS = [("add", 3, PREV), ("turn_x", 4, NEXT), ("route", 5, NEXT), ("turn_w", 11, NEXT)]
    STEPS += [("turn_n", 12, PREV), ("q", 13, PREV), ("k", 13, PREV), ("v", 13, PREV)] if qkv else []
    PROJ_BANK = {"q": MISC_BANK, "k": 6, "v": 5}
    N_NEXT = sum(s[2] == NEXT for s in STEPS)
    N_PREV = len(STEPS) - N_NEXT

    def there(step, c):
        if not isinstance(c, int):
            return True
        return c >= 1 if step[2] == PREV else c <= CHUNKS - 2

    def before(c):
        if isinstance(c, int) and c < 1:
            return 0 if c < 0 else N_NEXT
        if isinstance(c, int) and c == CHUNKS:
            return before(c - 1) + N_PREV
        return 2 * N_NEXT + (c - 1) * (N_NEXT + N_PREV)

    def count(name, c):
        return before(c) + ([s[0] for s in STEPS if there(s, c)].index(name) + 1)

    def on_chunks(eng, slot):
        for p in range(PAIRS):
            slot(0, 0, p)
        with eng.Fori(0, (CHUNKS - 2) // UNROLL) as k:
            for u in range(1, 1 + UNROLL):
                for p in range(PAIRS):
                    slot(k * UNROLL + u, u % 2, p)
        for p in range(PAIRS):
            slot(CHUNKS - 1, (CHUNKS - 1) % 2, p)

    def steps_at(c, p, late):
        return [s[0] for s in STEPS if s[1] == p - late and there(s, c)]

    SETUP = setup.steps if setup else {}

    y_half = sem("y_half")
    add_half = sem("add_half")
    final_half = sem("final_half")
    HALVES = [(h, slice(h * CHUNK // 2, (h + 1) * CHUNK // 2), range(h * TILES // 2, (h + 1) * TILES // 2))
              for h in range(2)]
    ADD_BANKS, TURN_BANKS, LAST_BANKS = (7, 3), (0, 1), {"q": 2, "k": 6, "v": 5}
    if qkv:
        mv_half = sem("mv_half")
        rstd_half = sem("rstd_half")
        xn_half = sem("xn_half")
        turn_half = sem("turn_half")
        x2_half = sem("x2_half")
        x2_lo_half = sem("x2_lo_half")
        last_ready = sem("last_ready")
        last_read = sem("last_read")

    def setup_at(c, p):
        return [n for n, at in SETUP.items() if at == p >= 0] if is_first(c) else []

    def is_first(c):
        return isinstance(c, int) and c == 0

    def at_start(c, p):
        return bool(setup) and is_first(c) and p < GROUP

    def tensor(pe):
        ident = w["ident"]

        def three(dst, hi, lo, x_hi, x_lo, start, stop):
            pe.matmul(dst, hi, x_hi, start=start, stop=False)
            pe.matmul(dst, hi, x_lo, start=False, stop=False)
            return pe.matmul(dst, lo, x_hi, start=False, stop=stop)

        def keep_warm(n, free_bank):
            for _ in range(n):
                pe.matmul(bank[:, free_bank, 0:P], ident[:], ident[:], start=True, stop=True)

        def down(c, p):
            g = PAIRS * c + p
            if p == 0:
                after(pe, y_made, c)
            after(pe, hi_made, g + 1)
            after(pe, lo_made, g + 1)
            if setup and is_first(c) and p % 4 == 0:
                pe.wait_ge(setup.passed, setup.number[f"dn{p // 4}"])
            b = p % HSPLIT
            three(y_bank, w["d_hi"][:, p, :], w["d_lo"][:, p, :], hid_hi[:, b, :], hid_lo[:, b, :],
                  p == 0, p == PAIRS - 1).then_inc(down_done, 1)

        def step(name, c, par):
            nxt = 1 - par
            after(pe, misc_read, count("turn_n", c) if name in ("k", "v") else count(name, c) - 1)
            if name == "add":
                after(pe, y_made, c)
                for i in range(TILES):
                    last = pe.transpose(misc[:, i * P:i * P + P], y_sb[:, i * P:i * P + P], ident[:])
            elif name in ("turn_x", "turn_n"):
                ln, k = (ln_f, c + 2) if name == "turn_x" else (ln_q, c)
                after(pe, ln["xn_made"], 2 * k)
                for i in range(TILES):
                    last = pe.transpose(misc[:, i * P:i * P + P], ln["xn"][:, i, :], ident[:])
            elif name == "route":
                for i in range(TILES):
                    s = slice(i * P, i * P + P)
                    o = misc[:, 2 * i * EXPERTS:2 * (i + 1) * EXPERTS]
                    pe.matmul(o, x_t[:, nxt, 0, s], w["r"][:].rearrange("h a e -> h (a e)"), start=True, stop=True)
                    last = pe.matmul(o[:, 0:EXPERTS], x_t[:, nxt, 1, s], w["r"][:, 0, :], start=False, stop=True,
                                     skip_group_check=True)
            elif name in "qkv":
                m = "qkv".index(name)
                last = three(bank[:, PROJ_BANK[name], :], w["qkv"][:, 0, m * P:m * P + P],
                             w["qkv"][:, 1, m * P:m * P + P], x2_t[:, 0, :], x2_t[:, 1, :], True, True)
            elif name == "turn_w":
                after(pe, wn_made, c + 2)
                last = pe.transpose(misc[:, 0:P], wn[:].rearrange("p a b -> p (a b)"), ident[:])
            last.then_inc(misc_ready, 1)

        def spread(p):
            if p == 0:
                pe.wait_ge(setup.sel_step, 3)
                pe.wait_ge(misc_read, count("turn_w", -1))
            after(pe, share_in[0], SHARE // GROUP * (p - 1))
            for i in range(TILES):
                last = pe.matmul(bank[:, SPREAD_BANKS[p % 2], i * P:i * P + P], setup.sel[:, TILES * p + i, :],
                                 comb_t[:], start=True, stop=True)
            last.then_inc(spread_ready, 1)

        def up_and_gate(c, par, p):
            g = PAIRS * c + p
            b = p % 2
            x_hi, x_lo = x_t[:, par, 0, :], x_t[:, par, 1, :]
            if p == 0:
                after(pe, misc_read, count("turn_x", -1) if at_start(c, p) else before(c))
            after(pe, scaled_made, g - 1)
            three(bank[:, UP_BANK + b, :], w["u_hi"][:, p, :], w["u_lo"][:, p, :],
                  x_hi, x_lo, True, True).then_inc(up_ready, 1)
            after(pe, hid_made, g - 1)
            three(bank[:, GATE_BANK + b, :], w["g_hi"][:, p, :], w["g_lo"][:, p, :],
                  x_hi, x_lo, True, True).then_inc(gate_ready, 1)

        def slot(c, par, p):
            if at_start(c, p) and p >= 2:
                spread(p)
            if setup and is_first(c) and p == GROUP:
                pe.wait_ge(share_in[0], SHARE)
            if setup and is_first(c) and p % 2 == 0:
                pe.wait_ge(setup.passed, setup.number[f"gu{p // 2}"])
            up_and_gate(c, par, p)
            if at_start(c, p) and p == 1:
                step("turn_w", -1, 1)
                keep_warm(4, Y_BANK)
                spread(0)
                spread(1)
                keep_warm(10, Y_BANK)
            if p >= LAG:
                down(c, p - LAG)
            elif not is_first(c):
                down(c - 1, PAIRS - LAG + p)
            for name in setup_at(c, p):
                setup.tensor(pe, name)
            for name in steps_at(c, p, 0):
                step(name, c, par)

        def tail():
            pe.wait_ge(misc_read, before(CHUNKS))
            for h, s, tiles in HALVES:
                pe.wait_ge(y_half, h + 1)
                for i in tiles:
                    last = pe.transpose(bank[:, ADD_BANKS[h], i * P:i * P + P], y_sb[:, i * P:i * P + P], ident[:])
                last.then_inc(add_half, 1)
            if not qkv:
                return
            keep_warm(14, LAST_BANKS["q"])
            for h, s, tiles in HALVES:
                pe.wait_ge(xn_half, h + 1)
                for i in tiles:
                    last = pe.transpose(bank[:, TURN_BANKS[h], i * P:i * P + P], ln_q["xn"][:, i, :], ident[:])
                last.then_inc(turn_half, 1)
            for h, s, tiles in HALVES:
                pe.wait_ge(x2_lo_half, h + 1)
                for m, name in enumerate("qkv"):
                    last = three(bank[:, LAST_BANKS[name], s], w["qkv"][:, 0, m * P:m * P + P],
                                 w["qkv"][:, 1, m * P:m * P + P], x2_t[:, 0, s], x2_t[:, 1, s], True, True)
                    if h == 1:
                        last.then_inc(last_ready, 1)
            keep_warm(16, Y_BANK)

        def ahead(*names):
            for name in names:
                if isinstance(name, str) and name[:5] == "read ":
                    pe.wait_ge(misc_read, count(name[5:], -1))
                elif isinstance(name, int):
                    pe.wait_ge(setup.const_step, 2)
                    keep_warm(name, Y_BANK)
                elif name in SETUP:
                    setup.tensor(pe, name)
                else:
                    step(name, -1, 1)

        def main():
            on_chunks(pe, slot)
            for p in range(PAIRS - LAG, PAIRS):
                down(CHUNKS - 1, p)
            tail()

        return Parts(ahead, main)

    def scalar(act):
        def copy_y(c):
            after(act, down_done, PAIRS * c)
            act.activation(y_sb[:], y_bank, ACT.Copy).then_inc(y_made, 1)

        def read(name, c, par):
            n = count(name, c)
            nxt = 1 - par
            if name == "turn_x":
                after(act, misc_ready, n)
                act.activation(x_t[:, nxt, 0, :], misc, ACT.Copy).then_inc(misc_half, 1)
            elif name == "turn_w":
                after(act, misc_ready, n)
                after(act, comb_stored, 16 * (c + 1))
                act.activation(comb_t[:], misc[:, 0:P], ACT.Copy).then_inc(misc_read, 1)
            elif name == "turn_n":
                after(act, misc_ready, n)
                act.activation(x2_t[:, 0, :], misc, ACT.Copy).then_inc(x2_hi_made, 1)
            elif name in ("q", "k", "v"):
                hold(act, proj_stats_made, 3 * (c - 1) + "qkv".index(name) + 1)
                act.activation(rows(qkv[name], c - 1).rearrange("p a b -> p (a b)"),
                               bank[:, PROJ_BANK[name], :], ACT.Copy).then_inc(misc_read, 1)

        def split_hi(g, p):
            after(act, hid_made, g + 1)
            after(act, down_done, g + 1 - HSPLIT)
            act.activation(hid_hi[:, p % HSPLIT, :], hid[:, p % 2, :], ACT.Copy).then_inc(hi_made, 1)

        def ln_apply(chunk, part):
            hold(act, shift_made, chunk + 1)
            x = rows(x_sb, chunk)
            for i in range(part * TILES // 2, (part + 1) * TILES // 2):
                last = act.activation(ln_q["xn"][:, i, :], x[:, i, :], ACT.Identity, scale=ln_q["rstd"][:, i, :],
                                      bias=ln_q["shift"][:, i, :])
            last.then_inc(ln_q["xn_made"], 1)

        def tail():
            if qkv:
                act.activation(w["nothing_s"][:], w["eps"][:, 0, :], ACT.Exp)
            act.wait_ge(down_done, PAIRS * CHUNKS)
            act.wait_ge(misc_ready, count("add", CHUNKS - 1))
            for h, s, tiles in HALVES:
                act.activation(y_sb[:, s], y_bank[:, s], ACT.Copy).then_inc(y_half, 1)
            if not qkv:
                return
            for h, s, tiles in HALVES:
                act.wait_ge(turn_half, h + 1)
                act.activation(x2_t[:, 0, s], bank[:, TURN_BANKS[h], s], ACT.Copy).then_inc(x2_half, 1)
            for m, name in enumerate("qkv"):
                act.wait_ge(proj_stats_made, 3 * (CHUNKS - 1) + m + 1)
                act.activation(rows(qkv[name], CHUNKS - 1).rearrange("p a b -> p (a b)"),
                               bank[:, LAST_BANKS[name], :], ACT.Copy).then_inc(last_read, 1)

        def tanh_z(k):
            after(act, z_made, k + 1)
            act.activation(th[:], z[:], ACT.Tanh, scale=0.5).then_inc(th_made, 1)

        def exp_z():
            act.wait_ge(z_made, 1)
            act.activation(th[:], z[:], ACT.Exp).then_inc(th_made, 1)

        def slot(c, par, p):
            g = PAIRS * c + p
            for name in setup_at(c, p - 1):
                setup.scalar(act, name)
            for name in steps_at(c, p, 1):
                read(name, c, par)
            follows = not isinstance(c, int) or c < CHUNKS - 1
            if follows and p == 7:
                tanh_z(c + 1)
            if qkv and not is_first(c) and p in (9, 10):
                ln_apply(c - 1, p - 9)
            after(act, gate_ready, g + 1)
            gate_bank = bank[:, GATE_BANK + p % 2, :]
            act.activation(gate_bank, gate_bank, ACT.Silu).then_inc(silu_made, 1)
            if p == PAIRS - 1:
                for name in setup_at(c, p):
                    setup.scalar(act, name)
            if at_start(c, p):
                if p == 0:
                    read("turn_w", -1, 1)
                act.wait_ge(spread_ready, p + 1)
                act.activation(share[:, 0, p, :], bank[:, SPREAD_BANKS[p % 2], :],
                               ACT.Copy).then_inc(share_in[0], SHARE // GROUP)
            if p == LAG - 1 and not is_first(c):
                copy_y(c)
            if not (is_first(c) and p == 0):
                split_hi(g - 1, (p - 1) % PAIRS)

        def ahead(*names):
            for name in names:
                if name == "silu":
                    if setup:
                        act.wait_ge(setup.const_step, 4)
                    act.activation(w["nothing_s"][:], w["eps"][:, 0, :], ACT.Silu)
                elif name == "tanh":
                    tanh_z(0)
                elif name == "exp":
                    exp_z()
                elif name in SETUP:
                    setup.scalar(act, name)
                else:
                    read(name, -1, 1)

        def main():
            on_chunks(act, slot)
            split_hi(PAIRS * CHUNKS - 1, PAIRS - 1)
            tail()

        return Parts(ahead, main)

    def vector(dve):
        late = None
        def ln_stats(ln, chunk, k, also=None, part=None):
            if also is not None:
                hold(dve, misc_read, also)
            elif setup and isinstance(chunk, int) and chunk < 2:
                dve.wait_ge(setup.x_in[chunk], 16)
            x = rows(x_sb, chunk)
            tiles = range(TILES) if part is None else range(part * TILES // 2, (part + 1) * TILES // 2)
            for i in tiles:
                last = dve.bn_stats(ln["stats"][:, i, :], x[:, i, :])
            if part == 0:
                return
            last.then_inc(ln["stats_made"], 1)
            hold(dve, ln["stats_made"], k + 1)
            for i in range(TILES):
                last = dve.bn_aggr(ln["mv"][:, i, :], ln["stats"][:, i, :])
            last.then_inc(ln["mv_made"], 1)

        def ln_apply(ln, chunk, k, part):
            hold(dve, ln["rstd_made"], k + 1)
            x = rows(x_sb, chunk)
            for i in range(part * TILES // 2, (part + 1) * TILES // 2):
                last = dve.tensor_scalar(ln["xn"][:, i, :], x[:, i, :], ln["mv"][:, i, 0:1], ln["rstd"][:, i, :],
                                         ALU.subtract, ALU.mult)
            last.then_inc(ln["xn_made"], 1)

        def pick(c, part):
            k = c + 1
            if part == 1:
                for i in range(TILES):
                    last = dve.match_replace(rest[:, i, :], top[:, i, :], logits[:, i, :], MASKED)
                last.then_inc(rest_made, 1)
                after(dve, rest_made, k + 1)
                dve.tensor_tensor(chosen[:], logits[:], rest[:], ALU.not_equal).then_inc(chosen_made, 1)
                return
            after(dve, misc_ready, count("route", c))
            both = misc[:, 0:2 * TILES * EXPERTS].rearrange("p (a two e) -> p a e two", two=2, e=EXPERTS)
            dve.tensor_reduce(logits[:], both, AX_X, ALU.add).then_inc(misc_read, 1)
            hold(dve, misc_read, count("route", c))
            for i in range(TILES):
                last = dve.max(top[:, i, :], logits[:, i, :])
            last.then_inc(top_made, 1)
            after(dve, top_made, k + 1)
            dve.tensor_tensor(z[:], logits[:], top[:, :, 0:1].to_broadcast([P, TILES, EXPERTS]),
                              ALU.subtract).then_inc(z_made, 1)

        def weigh(c, part, exp=False):
            k = c + 1
            if part == 0 and exp:
                dve.memset(den[:], 1.0).then_inc(den_made, 1)
                dve.memset(den_inv[:], 1.0).then_inc(den_inv_made, 1)
                after(dve, th_made, k + 1)
                after(dve, chosen_made, k + 1)
                dve.tensor_tensor(num[:], th[:], chosen[:], ALU.mult).then_inc(num_made, 1)
            elif part == 0:
                after(dve, th_made, k + 1)
                dve.tensor_scalar(den[:], th[:], -1.0, 1.0, ALU.mult, ALU.add).then_inc(den_made, 1)
                after(dve, chosen_made, k + 1)
                dve.scalar_tensor_tensor(out=num[:], in0=th[:], scalar=1.0, in1=chosen[:],
                                         op0=ALU.add, op1=ALU.mult).then_inc(num_made, 1)
            elif part == 1 and not exp:
                after(dve, den_made, k + 1)
                dve.reciprocal(den_inv[:], den[:]).then_inc(den_inv_made, 1)
            elif part == 2:
                after(dve, num_made, k + 1)
                after(dve, den_inv_made, k + 1)
                dve.tensor_tensor(wt[:], num[:], den_inv[:], ALU.mult).then_inc(wt_made, 1)
                after(dve, wt_made, k + 1)
                dve.tensor_reduce(wsum[:], wt[:], AX_X, ALU.add).then_inc(wsum_made, 1)
                after(dve, wsum_made, k + 1)
                dve.reciprocal(winv[:], wsum[:]).then_inc(winv_made, 1)
                after(dve, winv_made, k + 1)
                dve.scalar_tensor_tensor(out=wn[:], in0=wt[:], scalar=0.5,
                                         in1=winv[:].to_broadcast([P, TILES, EXPERTS]),
                                         op0=ALU.mult, op1=ALU.mult).then_inc(wn_made, 1)

        def read(name, c, par):
            n = count(name, c)
            nxt = 1 - par
            if name == "add":
                x = rows(x_sb, c - 1)
                after(dve, misc_ready, n)
                dve.tensor_tensor(x, misc.rearrange("p (a b) -> p a b", a=TILES), x,
                                  ALU.add).then_inc(misc_read, 1)
            elif name == "turn_x":
                after(dve, misc_half, c + 2)
                dve.tensor_tensor(x_t[:, nxt, 1, :], misc, x_t[:, nxt, 0, :].bitcast(F32),
                                  ALU.subtract).then_inc(misc_read, 1)
            elif name == "turn_n":
                after(dve, x2_hi_made, c)
                dve.tensor_tensor(x2_t[:, 1, :], misc, x2_t[:, 0, :].bitcast(F32),
                                  ALU.subtract).then_inc(misc_read, 1)
            elif name == "route":
                pick(c, 0)
            elif name in ("q", "k", "v"):
                m = "qkv".index(name)
                hold(dve, misc_ready, n)
                at = c - 1 + CHUNKS * m
                dst = w["proj_stats"][:, at, :] if isinstance(at, int) else w["proj_stats"][:, bass.ds(at, 1), :]
                dve.bn_stats(dst, bank[:, PROJ_BANK[name], :]).then_inc(proj_stats_made, 1)

        def tail():
            p, g = PAIRS - 1, PAIRS * CHUNKS
            dve.wait_ge(hi_made, g)
            dve.wait_ge(lo_made, g - 1)
            dve.tensor_tensor(hid_lo[:, p % HSPLIT, :], hid[:, p % 2, :], hid_hi[:, p % HSPLIT, :].bitcast(F32),
                              ALU.subtract).then_inc(lo_made, 1)
            x = rows(x_sb, CHUNKS - 1)
            for h, s, tiles in HALVES:
                dve.wait_ge(add_half, h + 1)
                a = slice(tiles[0], tiles[-1] + 1)
                dve.tensor_tensor(x[:, a, :], bank[:, ADD_BANKS[h], s].rearrange("p (a b) -> p a b", b=P),
                                  x[:, a, :], ALU.add).then_inc(final_half, 1)
                if not qkv:
                    continue
                dve.wait_ge(final_half, h + 1)
                for i in tiles:
                    last = dve.bn_stats(ln_q["stats"][:, i, :], x[:, i, :])
                last.then_inc(ln_q["stats_made"], 1)
                dve.wait_ge(ln_q["stats_made"], CHUNKS + h)
                for i in tiles:
                    last = dve.bn_aggr(ln_q["mv"][:, i, :], ln_q["stats"][:, i, :])
                last.then_inc(mv_half, 1)
            if not qkv:
                return
            for h, s, tiles in HALVES:
                dve.wait_ge(rstd_half, h + 1)
                for i in tiles:
                    last = dve.tensor_scalar(ln_q["xn"][:, i, :], x[:, i, :], ln_q["mv"][:, i, 0:1],
                                             ln_q["rstd"][:, i, :], ALU.subtract, ALU.mult)
                last.then_inc(xn_half, 1)
            for h, s, tiles in HALVES:
                dve.wait_ge(x2_half, h + 1)
                dve.tensor_tensor(x2_t[:, 1, s], bank[:, TURN_BANKS[h], s], x2_t[:, 0, s].bitcast(F32),
                                  ALU.subtract).then_inc(x2_lo_half, 1)
            for m, name in enumerate("qkv"):
                dve.wait_ge(last_ready, m + 1)
                dve.bn_stats(w["proj_stats"][:, CHUNKS - 1 + CHUNKS * m, :],
                             bank[:, LAST_BANKS[name], :]).then_inc(proj_stats_made, 1)

        def slot(c, par, p):
            g = PAIRS * c + p
            b = p % 2
            for name in setup_at(c, p - 1):
                setup.vector(dve, name)
            for name in steps_at(c, p, 1):
                read(name, c, par)
            follows = not isinstance(c, int) or c < CHUNKS - 1
            if p == 2 and is_first(c) and late:
                late()
            if follows and p == 0 and not (is_first(c) and late):
                ln_stats(ln_f, c + 1, c + 1)
            if setup and is_first(c) and p == PAIRS - 1:
                dve.wait_ge(setup.x_in[2], 16)
            if follows and p in (2, 3):
                ln_apply(ln_f, c + 1, c + 1, p - 2)
            if follows and p == 7:
                pick(c, 1)
            if follows and p in (8, 9, 10):
                weigh(c, p - 8)
            if qkv and not is_first(c):
                if p in (5, 6):
                    ln_stats(ln_q, c - 1, c - 1, count("add", c), p - 5)
                if p == 8:
                    after(dve, ln_q["rstd_made"], c)
                    dve.scalar_tensor_tensor(out=ln_q["shift"][:], in0=ln_q["mv"][:, :, 0:1], scalar=-1.0,
                                             in1=ln_q["rstd"][:], op0=ALU.mult,
                                             op1=ALU.mult).then_inc(shift_made, 1)
            q = p // GROUP
            if at_start(c, p):
                dve.wait_ge(share_in[0], SHARE // GROUP * (p + 1))
            elif p % GROUP == 0:
                after(dve, share_in[q % 2], SHARE * (2 * c + q // 2 + 1))
            after(dve, up_ready, g + 1)
            after(dve, hid_made, g - 1)
            dve.tensor_tensor(scaled[:, b, :], bank[:, UP_BANK + b, :],
                              share[:, p // GROUP % 2, p % GROUP, :], ALU.mult).then_inc(scaled_made, 1)
            after(dve, scaled_made, g + 1)
            after(dve, silu_made, g + 1)
            after(dve, lo_made, g - 1)
            dve.tensor_tensor(hid[:, b, :], bank[:, GATE_BANK + b, :], scaled[:, b, :],
                              ALU.mult).then_inc(hid_made, 1)
            if p == PAIRS - 1:
                for name in setup_at(c, p):
                    setup.vector(dve, name)

        def ahead(*names):
            for name in names:
                if name == "stats":
                    if final is not None:
                        dve.wait_ge(final, 1)
                    ln_stats(ln_f, 0, 0)
                elif name == "next stats":
                    dve.wait_ge(final, 2)
                    ln_stats(ln_f, 1, 1)
                elif name == "apply":
                    for part in range(2):
                        ln_apply(ln_f, 0, 0, part)
                elif name in ("weigh", "weigh_exp"):
                    for part in range(3):
                        weigh(-1, part, name == "weigh_exp")
                elif name == "route":
                    pick(-1, 0)
                    pick(-1, 1)
                elif name in SETUP:
                    setup.vector(dve, name)
                else:
                    read(name, -1, 1)

        def main(last_part=None):
            nonlocal late
            late = last_part
            on_chunks(dve, slot)
            tail()

        return Parts(ahead, main)

    def gpsimd(pool):
        def rstd(ln, k):
            after(pool, ln["mv_made"], k + 1)
            pool.tensor_tensor(ln["ve"][:], ln["mv"][:, :, 1:2], w["eps"][:], ALU.add).then_inc(ln["ve_made"], 1)
            after(pool, ln["ve_made"], k + 1)
            pool.tensor_tensor(ln["rstd"][:], ln["ve"][:], w["neg_half"][:], ALU.pow).then_inc(ln["rstd_made"], 1)

        def slot(c, par, p):
            g = PAIRS * c + p
            follows = not isinstance(c, int) or c < CHUNKS - 1
            if not follows and p == PAIRS - 1:
                return
            if follows and p == 0:
                rstd(ln_f, c + 1)
            if qkv and not is_first(c) and p == 6:
                rstd(ln_q, c - 1)
            after(pool, hi_made, g + 1)
            pool.tensor_tensor(hid_lo[:, p % HSPLIT, :], hid[:, p % 2, :],
                               hid_hi[:, p % HSPLIT, :].bitcast(F32), ALU.subtract).then_inc(lo_made, 1)

        def ahead():
            rstd(ln_f, 0)

        def main():
            on_chunks(pool, slot)
            if qkv:
                for h, s, tiles in HALVES:
                    a = slice(tiles[0], tiles[-1] + 1)
                    pool.wait_ge(mv_half, h + 1)
                    pool.tensor_tensor(ln_q["ve"][:, a, :], ln_q["mv"][:, a, 1:2], w["eps"][:, a, :],
                                       ALU.add).then_inc(ln_q["ve_made"], 1)
                    pool.wait_ge(ln_q["ve_made"], CHUNKS + h)
                    pool.tensor_tensor(ln_q["rstd"][:, a, :], ln_q["ve"][:, a, :], w["neg_half"][:, a, :],
                                       ALU.pow).then_inc(rstd_half, 1)

        return Parts(ahead, main)

    def sync(sp):
        def send_comb(k, par):
            hold(sp, misc_read, count("turn_w", k - 1))
            sp.dma_start(comb_d[par].rearrange("e (i t) -> i e t", i=TILES), comb_t[:]).then_inc(comb_stored, 16)

        def spread(c, par, q):
            if q == 0:
                hold(sp, comb_stored, 16 * (c + 1))
            hold(sp, scaled_made, PAIRS * c + GROUP * (q - 1))
            for half in range(2):
                src = comb_d[par].rearrange("(n two) t -> two n t", two=2)[half, GROUP * q:GROUP * q + GROUP, :]
                sp.dma_start(share[half * EDIM:half * EDIM + EDIM, q % 2, :, :],
                             src.partition_broadcast(EDIM)).then_inc(share_in[q % 2], 16)

        def store(c):
            hold(sp, misc_read, count("add", c))
            dst = out[c - 1] if isinstance(c, int) else out[bass.ds(c - 1, 1)].rearrange("a t h -> (a t) h")
            sp.dma_start(dst.rearrange("(n p) h -> p n h", p=P), rows(x_sb, c - 1)).then_inc(stored, 16)

        def chunk(c, par):
            spread(c, par, 2)
            if out is not None and not is_first(c):
                store(c)
            spread(c, par, 3)
            if not isinstance(c, int) or c < CHUNKS - 1:
                send_comb(c + 1, 1 - par)
                spread(c + 1, 1 - par, 0)
                spread(c + 1, 1 - par, 1)

        def main():
            send_comb(0, 0)
            if not setup:
                spread(0, 0, 0)
            else:
                sp.wait_ge(comb_stored, 16)
            spread(0, 0, 1)
            chunk(0, 0)
            with sp.Fori(0, (CHUNKS - 2) // UNROLL) as k:
                for u in range(1, 1 + UNROLL):
                    chunk(k * UNROLL + u, u % 2)
            chunk(CHUNKS - 1, (CHUNKS - 1) % 2)
            if out is not None:
                for h, s, tiles in HALVES:
                    a = slice(tiles[0], tiles[-1] + 1)
                    sp.wait_ge(final_half, h + 1)
                    sp.dma_start(out[CHUNKS - 1, s].rearrange("(n p) h -> p n h", p=P),
                                 rows(x_sb, CHUNKS - 1)[:, a, :]).then_inc(stored, 16)
                sp.wait_ge(stored, 16 * (CHUNKS + 1))

        return Parts(None, main)

    phase = Phase(tensor, scalar, vector, gpsimd, sync)
    if qkv:
        phase.proj_stats_made, phase.all_read, phase.reads = proj_stats_made, last_read, 3
    return phase


def attention_phase(ctx, nc, w, x_sb, bank, buf, qkv, before_it):
    def sb(name, shape, dt=F32):
        return ctx.enter_context(nc.sbuf_tensor(name, shape, dt))

    def sem(name):
        return ctx.enter_context(nc.semaphore(name))

    bn_mv = sb("bn_mv", [P, 3, 2])
    bn_ve = sb("bn_ve", [P, 3, 1])
    bn_rstd = sb("bn_rstd", [P, 3, 1])
    bn_scale = sb("bn_scale", [P, 3])
    bn_mean = sb("bn_mean", [P, 3])
    bn_shift = sb("bn_shift", [P, 3])
    q_scale = sb("q_scale", [P, 1])
    q_shift = sb("q_shift", [P, 1])
    v_shift = sb("v_shift", [P, P])
    out_v = sb("out_v", [P, P])
    shift_row = sb("shift_row", [P, P])
    q_n, v_f = buf["ln_q"]["xn"][:].rearrange("p a b -> p (a b)"), buf["y_sb"]
    k_n = sb("k_n", [P, CHUNK])[:]
    v_o = sb("v_o", [P, TILES, P])
    probs = sb("probs", [P, TILES, CHUNK])
    probs_t = sb("probs_t", [P, TILES, CHUNK])
    low = sb("low", [P, TILES])
    psum_row = sb("psum_row", [P, TILES])
    inv_row = sb("inv_row", [P, TILES])

    bn_step = sem("bn_step")
    bn_ve_made = sem("bn_ve_made")
    bn_rstd_made = sem("bn_rstd_made")
    shift_ready = sem("shift_ready")
    shift_made = sem("shift_made")
    shift_added = sem("shift_added")
    q_made = sem("q_made")
    k_made = sem("k_made")
    v_made = sem("v_made")
    s_ready = sem("s_ready")
    low_made = sem("low_made")
    exp_made = sem("exp_made")
    t_ready = sem("t_ready")
    even_made = sem("even_made")
    odd_made = sem("odd_made")
    y_ready = sem("y_ready")
    vo_ready = sem("vo_ready")
    vo_made = sem("vo_made")
    inv_made = sem("inv_made")
    x_done = sem("x_done")
    T_BANK, Y_BANK, V_BANK = 4, 6, 7
    y_bank = bank[:, Y_BANK, :]
    v_bank = bank[:, V_BANK, :]
    SCALE = float(P) ** -0.5

    def on_rows(eng, part, ahead):
        for b in (-1, 0):
            part(b)
        with eng.Fori(1, CHUNKS // 2) as b:
            part(b)
        ahead("part 3 done")
        for b in range(CHUNKS // 2, CHUNKS):
            part(b)
            ahead(f"part {b} done")
        return lambda: part(CHUNKS)

    def midst(b, ahead):
        if isinstance(b, int) and CHUNKS // 2 <= b < CHUNKS:
            ahead(f"in part {b}")

    def runs(b):
        return not isinstance(b, int) or 0 <= b < CHUNKS

    def scored(b):
        return not isinstance(b, int) or b + 1 < CHUNKS

    def has_last(b):
        return not isinstance(b, int) or b >= 1

    def flat(t, b):
        return rows(t, b).rearrange("p a b -> p (a b)")

    def tensor(pe, ahead):
        pe.wait_ge(before_it.all_read, before_it.reads)
        pe.wait_ge(bn_step, 9)
        pe.matmul(y_bank[:, 0:P], v_shift[:], w["out_t"][:], start=True, stop=True).then_inc(shift_ready, 1)

        def turn(b, j):
            if j == 0:
                after(pe, exp_made, TILES * b + TILES)
            after(pe, (even_made, odd_made)[j % 2], 2 * b + j // 2)
            for i in range(j, TILES):
                last = pe.transpose(bank[:, T_BANK + j % 2, i * P:i * P + P], probs[:, i, j * P:j * P + P],
                                    w["ident"][:])
            last.then_inc(t_ready, 1)

        def scores(b, i):
            if i == 0:
                after(pe, q_made, b + 1)
                after(pe, k_made, b + 1)
            after(pe, exp_made, TILES * (b - 1) + i + 1)
            n = i * P + P
            if i:
                pe.matmul(bank[:, i, 0:i * P], q_n[:, i * P:n], k_n[:, 0:i * P], start=True, stop=True)
            pe.matmul(bank[:, i, i * P:n], q_n[:, i * P:n], k_n[:, i * P:n], start=True, stop=False)
            pe.matmul(bank[:, i, i * P:n], w["ident_b"][:], w["causal_b"][:], start=False,
                      stop=True).then_inc(s_ready, 1)

        def part(b):
            if runs(b):
                turn(b, 0)
                turn(b, 1)
                if isinstance(b, int):
                    ahead(f"row {b}'s v")
                after(pe, v_made, b + 1)
                after(pe, vo_made, b)
                for i in range(TILES):
                    last = pe.matmul(v_bank[:, i * P:i * P + P], v_f[:, i * P:i * P + P], out_v[:],
                                     start=True, stop=True)
                last.then_inc(vo_ready, 1)
            if scored(b):
                scores(b + 1, 0)
                scores(b + 1, 1)
            if runs(b):
                turn(b, 2)
                turn(b, 3)
            if scored(b):
                scores(b + 1, 2)
                scores(b + 1, 3)
            if runs(b):
                after(pe, vo_made, b + 1)
            midst(b, ahead)
            if isinstance(b, int) and b == 0:
                pe.wait_ge(shift_made, 1)
            if runs(b):
                after(pe, x_done, b)
                for i in range(TILES):
                    after(pe, (even_made, odd_made)[i % 2], 2 * b + i // 2 + 1)
                    for j in range(i + 1):
                        last = pe.matmul(y_bank[:, i * P:i * P + P], probs_t[:, j, i * P:i * P + P], v_o[:, j, :],
                                         start=(j == 0), stop=(j == i))
                last.then_inc(y_ready, 1)

        return on_rows(pe, part, ahead)

    def scalar(act, ahead):
        act.wait_ge(bn_step, 9)

        def exps(b, i):
            after(act, low_made, TILES * b + i + 1)
            after(act, t_ready, TILES * (b - 1) + i + 1)
            after(act, inv_made, b)
            n = i * P + P
            act.activation(probs[:, i, 0:n], bank[:, i, 0:n], ACT.Exp, scale=-1.0, bias=low[:, i:i + 1],
                           accum_out=psum_row[:, i:i + 1]).then_inc(exp_made, 1)

        def odd(b, j):
            after(act, t_ready, TILES * b + j + 1)
            after(act, y_ready, b)
            act.activation(probs_t[:, j, j * P:CHUNK], bank[:, T_BANK + 1, j * P:CHUNK],
                           ACT.Copy).then_inc(odd_made, 1)

        def part(b):
            if scored(b):
                hold(act, s_ready, TILES * (b + 1))
                act.activation(q_n, flat(qkv["q"], b + 1), ACT.Identity, scale=q_scale[:],
                               bias=q_shift[:]).then_inc(q_made, 1)
            if not runs(b) and scored(b):
                act.wait_ge(shift_ready, 1)
                act.activation(shift_row[:], y_bank[:, 0:P], ACT.Copy).then_inc(shift_made, 1)
            if runs(b):
                odd(b, 1)
                after(act, vo_ready, b + 1)
                act.activation(v_o[:].rearrange("p a b -> p (a b)"), v_bank, ACT.Copy).then_inc(vo_made, 1)
            if scored(b):
                exps(b + 1, 0)
                exps(b + 1, 1)
            midst(b, ahead)
            if runs(b):
                odd(b, 3)
            if scored(b):
                exps(b + 1, 2)
                exps(b + 1, 3)

        on_rows(act, part, ahead)

    def vector(dve, ahead):
        dve.wait_ge(before_it.proj_stats_made, 3 * CHUNKS)
        for m in range(3):
            last = dve.bn_aggr(bn_mv[:, m, :], w["proj_stats"][:, m * CHUNKS:(m + 1) * CHUNKS, :])
        last.then_inc(bn_step, 1)
        dve.wait_ge(bn_rstd_made, 1)
        col = lambda t: t[:].rearrange("p (a b) -> p a b", b=1)
        dve.tensor_tensor(col(bn_scale), w["gamma_beta"][:, 0:3].rearrange("p (a b) -> p a b", b=1), bn_rstd[:],
                          ALU.mult).then_inc(bn_step, 1)
        dve.wait_ge(bn_step, 2)
        dve.tensor_tensor(col(bn_mean), bn_mv[:, :, 0:1], col(bn_scale), ALU.mult).then_inc(bn_step, 1)
        dve.wait_ge(bn_step, 3)
        dve.tensor_tensor(bn_shift[:], w["gamma_beta"][:, 3:6], bn_mean[:], ALU.subtract).then_inc(bn_step, 1)
        dve.wait_ge(bn_step, 4)
        dve.tensor_scalar(q_scale[:], bn_scale[:, 0:1], -SCALE, None, ALU.mult).then_inc(bn_step, 1)
        dve.tensor_scalar(q_shift[:], bn_shift[:, 0:1], -SCALE, None, ALU.mult).then_inc(bn_step, 1)
        dve.tensor_scalar(out_v[:], w["out_t"][:], bn_scale[:, 2:3], None, ALU.mult).then_inc(bn_step, 1)
        dve.tensor_copy(v_shift[:], bn_shift[:, 2:3].to_broadcast([P, P])).then_inc(bn_step, 1)
        dve.memset(low[:], 0.0).then_inc(bn_step, 1)
        dve.wait_ge(bn_step, 9)

        def even(b, j):
            after(dve, t_ready, TILES * b + j + 1)
            after(dve, y_ready, b)
            dve.tensor_copy(probs_t[:, j, j * P:CHUNK], bank[:, T_BANK, j * P:CHUNK]).then_inc(even_made, 1)

        def lows(b, i):
            after(dve, s_ready, TILES * b + i + 1)
            after(dve, exp_made, TILES * (b - 1) + i + 1)
            dve.tensor_reduce(low[:, i:i + 1], bank[:, i, 0:i * P + P], AX_X, ALU.min).then_inc(low_made, 1)

        def part(b):
            if scored(b):
                after(dve, s_ready, TILES * (b + 1))
                dve.tensor_scalar(k_n, flat(qkv["k"], b + 1), bn_scale[:, 1:2], bn_shift[:, 1:2],
                                  ALU.mult, ALU.add).then_inc(k_made, 1)
            if runs(b):
                even(b, 0)
            if has_last(b):
                dve.wait_ge(shift_added, 1)
                hold(dve, y_ready, b)
                hold(dve, inv_made, b)
                x = rows(x_sb, b - 1)
                for i in range(TILES):
                    last = dve.scalar_tensor_tensor(out=x[:, i, :], in0=y_bank[:, i * P:i * P + P],
                                                    scalar=inv_row[:, i:i + 1], in1=x[:, i, :],
                                                    op0=ALU.mult, op1=ALU.add)
                last.then_inc(x_done, 1)
            if runs(b):
                after(dve, exp_made, TILES * b + TILES)
                after(dve, x_done, b)
                dve.reciprocal(inv_row[:], psum_row[:]).then_inc(inv_made, 1)
            if scored(b):
                lows(b + 1, 0)
                lows(b + 1, 1)
            midst(b, ahead)
            if runs(b):
                even(b, 2)
            if scored(b):
                lows(b + 1, 2)
                lows(b + 1, 3)

        dve.wait_ge(before_it.all_read, before_it.reads)
        return on_rows(dve, part, ahead)

    def gpsimd(pool, ahead):
        pool.wait_ge(bn_step, 1)
        pool.tensor_tensor(bn_ve[:], bn_mv[:, :, 1:2], w["eps"][:, 0:3, :], ALU.add).then_inc(bn_ve_made, 1)
        pool.wait_ge(bn_ve_made, 1)
        pool.tensor_tensor(bn_rstd[:], bn_ve[:], w["neg_half"][:, 0:3, :], ALU.pow).then_inc(bn_rstd_made, 1)

        def copy_v(b):
            hold(pool, vo_ready, b)
            pool.tensor_copy(v_f[:], rows(qkv["v"], b).rearrange("p a b -> p (a b)")).then_inc(v_made, 1)

        pool.wait_ge(before_it.all_read, before_it.reads)
        copy_v(0)
        pool.wait_ge(shift_made, 1)
        pool.tensor_tensor(x_sb[:], x_sb[:], shift_row[:].rearrange("p (a b) -> p a b", a=1)
                           .to_broadcast([P, TILES * CHUNKS, P]), ALU.add).then_inc(shift_added, 1)
        with pool.Fori(1, CHUNKS // 2 + 1) as b:
            copy_v(b)
        ahead()
        with pool.Fori(CHUNKS // 2 + 1, CHUNKS) as b:
            copy_v(b)

    phase = Phase(tensor, scalar, vector, gpsimd, None)
    phase.x_done = x_done
    return phase


def build(nc, x, W_attn, W_proj, lora_attn_A, lora_attn_B, lora_proj_A, lora_proj_B, gamma, beta, gate, gate_up,
          down, out):
    d = {"x": x, "W_attn": W_attn, "W_proj": W_proj, "lora_attn_A": lora_attn_A, "lora_attn_B": lora_attn_B,
         "lora_proj_A": lora_proj_A, "lora_proj_B": lora_proj_B, "gamma": gamma, "beta": beta, "gate": gate,
         "gate_up": gate_up, "down": down}
    with ExitStack() as ctx:
        def sb(name, shape, dt=F32):
            return ctx.enter_context(nc.sbuf_tensor(name, shape, dt))

        bank = ctx.enter_context(nc.psum_tensor("bank", [P, 8, CHUNK], F32))
        x_sb = sb("x_sb", [P, CHUNKS * TILES, P])
        w = {n: sb(n, [P, PAIRS, P], F32R) for n in ("g_hi", "g_lo", "u_hi", "u_lo", "d_hi", "d_lo")}
        w["r"] = sb("r", [P, 2, EXPERTS], F32R)
        w["qkv"] = sb("qkv", [P, 2, 3 * P], F32R)
        w |= {"nothing": sb("nothing", [P, 1]), "nothing_s": sb("nothing_s", [P, 1]),
              "out_t": sb("out_t", [P, P]), "ident": sb("ident", [P, P]),
              "ident_b": sb("ident_b", [P, P], mybir.dt.bfloat16),
              "causal_b": sb("causal_b", [P, P], mybir.dt.bfloat16),
              "gamma_beta": sb("gamma_beta", [P, 6]),
              "eps": sb("eps", [P, TILES, 1]), "neg_half": sb("neg_half", [P, TILES, 1]),
              "proj_stats": sb("proj_stats", [P, 3 * CHUNKS, 6])}
        qkv = {n: sb(f"{n}_all", [P, CHUNKS * TILES, P]) for n in "qkv"}
        qkv |= {"x2_t": sb("x2_t", [P, 2, CHUNK], F32R)}
        buf = ffn_buffers(ctx, nc)
        setup = setup_phase(ctx, nc, d, w, x_sb, bank, qkv)
        ffn_a = ffn_phase(ctx, nc, "a", w, x_sb, bank, buf, qkv=qkv, setup=setup)
        attn = attention_phase(ctx, nc, w, x_sb, bank, buf, qkv, ffn_a)
        ffn_c = ffn_phase(ctx, nc, "c", w, x_sb, bank, buf, final=attn.x_done, out=out)
        block = ctx.enter_context(nc.Block())

        def between(parts, steps):
            return lambda place: parts.ahead(*steps.get(place, ()))

        @block.sync
        def _(sp):
            setup.sync(sp)
            ffn_a.sync(sp).main()
            ffn_c.sync(sp).main()

        @block.gpsimd
        def _(pool):
            setup.gpsimd(pool)
            a, c = ffn_a.gpsimd(pool), ffn_c.gpsimd(pool)
            a.ahead()
            setup.selectors(pool)
            a.main()
            attn.gpsimd(pool, c.ahead)
            c.main()

        @block.scalar
        def _(act):
            a, c = ffn_a.scalar(act), ffn_c.scalar(act)
            setup.loads(act)
            a.ahead("silu", "gate", "turn_x", "gu0", "tanh")
            a.main()
            attn.scalar(act, between(c, {"part 4 done": ["turn_x"], "part 5 done": ["exp"],
                                         "part 6 done": ["turn_w"]}))
            c.main()

        @block.vector
        def _(dve):
            dve.wait_ge(setup.const_step, 4)
            a, c = ffn_a.vector(dve), ffn_c.vector(dve)
            a.ahead("stats", "apply", "gate", "turn_x", "gu0", "route", "weigh")
            a.main()
            last = attn.vector(dve, between(c, {"part 3 done": ["stats"], "in part 4": ["apply"],
                                                "part 4 done": ["turn_x"], "part 5 done": ["route"],
                                                "in part 6": ["weigh_exp"], "part 7 done": ["next stats"]}))
            c.main(last)

        @block.tensor
        def _(pe):
            a, c = ffn_a.tensor(pe), ffn_c.tensor(pe)
            a.ahead(5, "gate", 7, "turn_x", "gu0", "route")
            a.main()
            attn.tensor(pe, between(c, {"part 4 done": ["turn_x"], "row 5's v": ["read turn_x"],
                                        "in part 5": ["route"], "row 6's v": ["read route"],
                                        "in part 6": ["turn_w"], "row 7's v": ["read turn_w"]}))
            c.main()


_INS = ["L0_attn_x", "L0_attn_W_attn", "L0_attn_W_proj", "L0_attn_lora_attn_A", "L0_attn_lora_attn_B",
        "L0_attn_lora_proj_A", "L0_attn_lora_proj_B", "L0_attn_bn_gamma", "L0_attn_bn_beta",
        "L0_ffn_gate_w", "L0_ffn_gate_up_w", "L0_ffn_down_w"]


def kernel(**inputs):
    import concourse.bacc as bacc
    from concourse.bass_utils import run_bass_kernel_spmd

    nc = bacc.Bacc("TRN2", target_bir_lowering=False, num_devices=1)
    arrays, args = {}, []
    for name in _INS:
        a = np.ascontiguousarray(inputs[name])
        arrays[name] = a
        args.append(nc.dram_tensor(name, a.shape, mybir.dt.from_np(a.dtype), kind="ExternalInput").ap())
    shape = arrays["L0_attn_x"].shape
    args.append(nc.dram_tensor("y_out", shape, F32, kind="ExternalOutput").ap())
    build(nc, *args)
    r = run_bass_kernel_spmd(nc, [arrays], core_ids=[0])
    return r.results[0]["y_out"]
```
